# Optimizing a Trainium2 kernel written in Bass

```python
import numpy as np
import jax
import jax.numpy as jnp

def _softmax(x, axis=-1):
    return jax.nn.softmax(x, axis=axis)

def _gelu(x):
    return jax.nn.gelu(x, approximate=True)

def _silu(x):
    return jax.nn.silu(x)

def _sigmoid(x):
    return jax.nn.sigmoid(x)

def _layernorm(x, axis=-1, eps=1e-05):
    m = jnp.mean(x, axis=axis, keepdims=True)
    v = jnp.var(x, axis=axis, keepdims=True)
    return (x - m) / jnp.sqrt(v + eps)

def _scatter_add(tgt, idx, src, axis=0):
    return tgt.at[idx].add(src)

def _segment_sum(src, seg, n):
    return jax.ops.segment_sum(src, seg, n)
kernel_name = 'mk_dlrm_tower_d1_rec_r8_5eaf27'

def setup_inputs(seed: int=0):
    np.random.seed(seed)
    _w = jnp.asarray

    def _rec_inputs():
        import jax
        import jax.numpy as jnp
        _tk = jax.random.key(seed)
        ids = jnp.stack([jax.random.randint(jax.random.fold_in(_tk, 200 + f), (2048,), 0, v, jnp.int32) for f, v in enumerate([125000, 1000, 1000, 12500, 12500, 1000, 1250, 1000, 1000, 1250, 1000, 1000, 12500, 12500, 1250, 1250, 1000, 1250, 12500, 12500, 1000, 1250, 1250, 1250, 1250, 12500])], axis=1)
        tbl_0 = 0.05 * jax.random.normal(jax.random.fold_in(_tk, 500 + 0), (125000, 128), jnp.float32)
        tbl_1 = 0.05 * jax.random.normal(jax.random.fold_in(_tk, 500 + 1), (1000, 128), jnp.float32)
        tbl_2 = 0.05 * jax.random.normal(jax.random.fold_in(_tk, 500 + 2), (1000, 128), jnp.float32)
        tbl_3 = 0.05 * jax.random.normal(jax.random.fold_in(_tk, 500 + 3), (12500, 128), jnp.float32)
        tbl_4 = 0.05 * jax.random.normal(jax.random.fold_in(_tk, 500 + 4), (12500, 128), jnp.float32)
        tbl_5 = 0.05 * jax.random.normal(jax.random.fold_in(_tk, 500 + 5), (1000, 128), jnp.float32)
        tbl_6 = 0.05 * jax.random.normal(jax.random.fold_in(_tk, 500 + 6), (1250, 128), jnp.float32)
        tbl_7 = 0.05 * jax.random.normal(jax.random.fold_in(_tk, 500 + 7), (1000, 128), jnp.float32)
        tbl_8 = 0.05 * jax.random.normal(jax.random.fold_in(_tk, 500 + 8), (1000, 128), jnp.float32)
        tbl_9 = 0.05 * jax.random.normal(jax.random.fold_in(_tk, 500 + 9), (1250, 128), jnp.float32)
        tbl_10 = 0.05 * jax.random.normal(jax.random.fold_in(_tk, 500 + 10), (1000, 128), jnp.float32)
        tbl_11 = 0.05 * jax.random.normal(jax.random.fold_in(_tk, 500 + 11), (1000, 128), jnp.float32)
        tbl_12 = 0.05 * jax.random.normal(jax.random.fold_in(_tk, 500 + 12), (12500, 128), jnp.float32)
        tbl_13 = 0.05 * jax.random.normal(jax.random.fold_in(_tk, 500 + 13), (12500, 128), jnp.float32)
        tbl_14 = 0.05 * jax.random.normal(jax.random.fold_in(_tk, 500 + 14), (1250, 128), jnp.float32)
        tbl_15 = 0.05 * jax.random.normal(jax.random.fold_in(_tk, 500 + 15), (1250, 128), jnp.float32)
        tbl_16 = 0.05 * jax.random.normal(jax.random.fold_in(_tk, 500 + 16), (1000, 128), jnp.float32)
        tbl_17 = 0.05 * jax.random.normal(jax.random.fold_in(_tk, 500 + 17), (1250, 128), jnp.float32)
        tbl_18 = 0.05 * jax.random.normal(jax.random.fold_in(_tk, 500 + 18), (12500, 128), jnp.float32)
        tbl_19 = 0.05 * jax.random.normal(jax.random.fold_in(_tk, 500 + 19), (12500, 128), jnp.float32)
        tbl_20 = 0.05 * jax.random.normal(jax.random.fold_in(_tk, 500 + 20), (1000, 128), jnp.float32)
        tbl_21 = 0.05 * jax.random.normal(jax.random.fold_in(_tk, 500 + 21), (1250, 128), jnp.float32)
        tbl_22 = 0.05 * jax.random.normal(jax.random.fold_in(_tk, 500 + 22), (1250, 128), jnp.float32)
        tbl_23 = 0.05 * jax.random.normal(jax.random.fold_in(_tk, 500 + 23), (1250, 128), jnp.float32)
        tbl_24 = 0.05 * jax.random.normal(jax.random.fold_in(_tk, 500 + 24), (1250, 128), jnp.float32)
        tbl_25 = 0.05 * jax.random.normal(jax.random.fold_in(_tk, 500 + 25), (12500, 128), jnp.float32)
        _rk = jax.random.fold_in(_tk, 7)
        r_dense_x = -0.000514642 + 1.00011 * jax.random.normal(jax.random.fold_in(_rk, 101), (2048, 128), jnp.float32)
        W_top1 = 0.0456912 * jax.random.normal(jax.random.fold_in(_tk, 801), (479, 512), jnp.float32)
        W_top2 = 0.0441942 * jax.random.normal(jax.random.fold_in(_tk, 802), (512, 256), jnp.float32)
        W_top3 = 0.0625 * jax.random.normal(jax.random.fold_in(_tk, 803), (256, 1), jnp.float32)
        b_top1 = jnp.zeros((512,), jnp.float32)
        b_top2 = jnp.zeros((256,), jnp.float32)
        return (r_dense_x, ids, tbl_0, tbl_1, tbl_2, tbl_3, tbl_4, tbl_5, tbl_6, tbl_7, tbl_8, tbl_9, tbl_10, tbl_11, tbl_12, tbl_13, tbl_14, tbl_15, tbl_16, tbl_17, tbl_18, tbl_19, tbl_20, tbl_21, tbl_22, tbl_23, tbl_24, tbl_25, W_top1, b_top1, W_top2, b_top2, W_top3)
    r_dense_x, ids, tbl_0, tbl_1, tbl_2, tbl_3, tbl_4, tbl_5, tbl_6, tbl_7, tbl_8, tbl_9, tbl_10, tbl_11, tbl_12, tbl_13, tbl_14, tbl_15, tbl_16, tbl_17, tbl_18, tbl_19, tbl_20, tbl_21, tbl_22, tbl_23, tbl_24, tbl_25, W_top1, b_top1, W_top2, b_top2, W_top3 = _rec_inputs()

    def _L0_rec_setup():
        import jax, jax.numpy as jnp
        import numpy as np
        F = 26
        D = 128
        B = 2048
        _TRIU_I, _TRIU_J = np.triu_indices(F + 1, k=1)
        _TRIU_I = jnp.asarray(_TRIU_I)
        _TRIU_J = jnp.asarray(_TRIU_J)
        key = jax.random.key(seed)
        k1, k2 = jax.random.split(key)
        sparse_x = jax.random.normal(k1, (B, F, D), dtype=jnp.float32)
        dense_x = jax.random.normal(k2, (B, D), dtype=jnp.float32)
        return {'sparse_x': sparse_x, 'dense_x': dense_x}
    _L0_rec_all = _L0_rec_setup()
    _L0_rec_in = {k: v for k, v in _L0_rec_all.items() if k in ()}
    del _L0_rec_all
    return {'r_dense_x': r_dense_x, 'ids': ids, 'tbl_0': tbl_0, 'tbl_1': tbl_1, 'tbl_2': tbl_2, 'tbl_3': tbl_3, 'tbl_4': tbl_4, 'tbl_5': tbl_5, 'tbl_6': tbl_6, 'tbl_7': tbl_7, 'tbl_8': tbl_8, 'tbl_9': tbl_9, 'tbl_10': tbl_10, 'tbl_11': tbl_11, 'tbl_12': tbl_12, 'tbl_13': tbl_13, 'tbl_14': tbl_14, 'tbl_15': tbl_15, 'tbl_16': tbl_16, 'tbl_17': tbl_17, 'tbl_18': tbl_18, 'tbl_19': tbl_19, 'tbl_20': tbl_20, 'tbl_21': tbl_21, 'tbl_22': tbl_22, 'tbl_23': tbl_23, 'tbl_24': tbl_24, 'tbl_25': tbl_25, 'W_top1': W_top1, 'b_top1': b_top1, 'W_top2': W_top2, 'b_top2': b_top2, 'W_top3': W_top3}

def reference(r_dense_x, ids, tbl_0, tbl_1, tbl_2, tbl_3, tbl_4, tbl_5, tbl_6, tbl_7, tbl_8, tbl_9, tbl_10, tbl_11, tbl_12, tbl_13, tbl_14, tbl_15, tbl_16, tbl_17, tbl_18, tbl_19, tbl_20, tbl_21, tbl_22, tbl_23, tbl_24, tbl_25, W_top1, b_top1, W_top2, b_top2, W_top3):
    import jax
    import jax.numpy as jnp

    def _L0_rec_ref(sparse_x, dense_x):
        import jax, jax.numpy as jnp
        import numpy as np
        F = 26
        D = 128
        B = 2048
        _TRIU_I, _TRIU_J = np.triu_indices(F + 1, k=1)
        _TRIU_I = jnp.asarray(_TRIU_I)
        _TRIU_J = jnp.asarray(_TRIU_J)
        combined = jnp.concatenate([sparse_x, dense_x[:, None, :]], axis=1)
        interact = jnp.einsum('bfd,bgd->bfg', combined, combined)
        return interact[:, _TRIU_I, _TRIU_J]
    e = jnp.stack([tbl_0[ids[:, 0]], tbl_1[ids[:, 1]], tbl_2[ids[:, 2]], tbl_3[ids[:, 3]], tbl_4[ids[:, 4]], tbl_5[ids[:, 5]], tbl_6[ids[:, 6]], tbl_7[ids[:, 7]], tbl_8[ids[:, 8]], tbl_9[ids[:, 9]], tbl_10[ids[:, 10]], tbl_11[ids[:, 11]], tbl_12[ids[:, 12]], tbl_13[ids[:, 13]], tbl_14[ids[:, 14]], tbl_15[ids[:, 15]], tbl_16[ids[:, 16]], tbl_17[ids[:, 17]], tbl_18[ids[:, 18]], tbl_19[ids[:, 19]], tbl_20[ids[:, 20]], tbl_21[ids[:, 21]], tbl_22[ids[:, 22]], tbl_23[ids[:, 23]], tbl_24[ids[:, 24]], tbl_25[ids[:, 25]]], axis=1)
    z = _L0_rec_ref(e, r_dense_x)
    z = z.reshape(z.shape[0], -1)
    h = jnp.concatenate([z, r_dense_x], axis=1)
    h = jnp.maximum(h @ W_top1 + b_top1, 0.0)
    h = jnp.maximum(h @ W_top2 + b_top2, 0.0)
    y = h @ W_top3
    return y

_drawn_inputs = setup_inputs


def setup_inputs(seed=0):
    import zlib

    import numpy as np

    out = dict(_drawn_inputs(seed))
    spreads = {'b_top1': (0.0, 0.1), 'b_top2': (0.0, 0.1)}
    factors = {}
    for name, (base, spread) in spreads.items():
        noise = np.random.default_rng([zlib.crc32(name.encode()), seed]).standard_normal(out[name].shape)
        drawn = base * np.exp(spread * noise) if base else spread * noise
        out[name] = jnp.asarray(drawn.astype(out[name].dtype))
    for name, factor in factors.items():
        out[name] = (out[name] * factor).astype(out[name].dtype)
    return out
```

```python
import concourse.bass as bass
from concourse import mybir
from contextlib import ExitStack


def dlrm_tower(nc, dense, ids, tables, w1, b1, w2, b2, w3, out):
    fp32, f32r = mybir.dt.float32, mybir.dt.float32r
    fp16, i32 = mybir.dt.float16, mybir.dt.int32
    ALU = mybir.AluOpType
    ACT = mybir.ActivationFunctionType

    P = 128
    B, D = dense.shape
    NF = len(tables)
    F = NF + 1
    FP = 32
    TILES = B // P
    SUPER = TILES // 2
    SB = 2 * P
    N1, N2 = w1.shape[1], w2.shape[1]
    PAIRS = F * (F - 1) // 2
    ZC = 3
    ZK = PAIRS // ZC
    QUADS = P // 4

    ONEHOT = [1, 2, 5, 7, 8, 10, 11, 16]
    GROUPS = [[0, 3, 6, 9], [12, 13, 14, 15], [17, 18, 19, 20], [21, 22, 23, 24], [4, 25, NF]]
    SLOTS = [f for group in GROUPS for f in group]
    GATHERED = SLOTS[:-1]
    NG, NO = len(GATHERED), len(ONEHOT)
    ROWS = tables[ONEHOT[0]].shape[0]
    CH = 8
    RP = ROWS // CH
    NP = NO // 2
    assert sorted(ONEHOT + SLOTS) == list(range(F)) and all(tables[f].shape[0] == ROWS for f in ONEHOT)

    def numbered(start, names):
        return {name: ((start + n) % 2, (start + n) // 2 + 1) for n, name in enumerate(names)}

    ID = [("ids", p) for p in range(NP)]
    LOOK = [("lookup", p) for p in range(NP)]
    ROWT = [[("rows", t, g) for g in range(len(GROUPS))] for t in range(2)]
    ORDER = ROWT[0] + [("z", 1)] + ID[0:2] + LOOK[0:2] + ID[2:4] + [("z", 0)] + ROWT[1] + LOOK[2:4]
    AHEAD = ID[0:2] + LOOK[0:2] + ID[2:4] + LOOK[2:4]
    PER = len(ORDER)
    BEFORE = numbered(0, AHEAD)
    first_order = [x for x in ORDER if x != ("z", 1)]
    last_order = [x for x in ORDER if x not in AHEAD]
    n1 = len(AHEAD) + len(first_order)
    FIRST = numbered(len(AHEAD), first_order)
    STEADY = numbered(n1, ORDER)
    LAST = numbered(n1 + PER * (SUPER - 2), last_order)
    AFTER = numbered(n1 + PER * (SUPER - 2) + len(last_order), [("z", 1)])
    assert PER % 2 == 0

    def fill_of(s, name):
        if isinstance(s, int):
            if s < 0:
                return BEFORE[name]
            if s == 0:
                return FIRST[name]
            if s == SUPER - 1:
                return LAST[name]
            if s == SUPER:
                return AFTER[name]
        bank, count = STEADY[name]
        return bank, (s - 1) * (PER // 2) + count

    ctx = ExitStack()
    with ctx:
        def sb(name, shape, dt):
            return ctx.enter_context(nc.sbuf_tensor(name, shape, dt))

        def pb(name, shape, dt):
            return ctx.enter_context(nc.psum_tensor(name, shape, dt))

        def sem(name):
            return ctx.enter_context(nc.semaphore(name))

        gather_ids = sb("gather_ids", [P, 2, NF], i32)
        ids_raw = sb("ids_raw", [P, TILES, NF], i32)
        ids_half = sb("ids_half", [P, TILES, NO], fp16)
        ids_rows = sb("ids_rows", [P, B], fp16)
        pick = sb("pick", [P, NO, P], fp16)
        ident = sb("ident", [P, P], fp32)
        ident16 = sb("ident16", [P, P], fp16)
        table_hi = sb("table_hi", [RP, NO, CH, D], f32r)
        table_lo = sb("table_lo", [RP, NO, CH, D], f32r)
        offsets = sb("offsets", [P, 2, 2, SB], fp16)
        onehot = sb("onehot", [RP, 2, CH, SB], f32r)
        rows = sb("rows", [P, 2, NG + 1, D], fp32)
        features = sb("features", [P, 2, SB, FP], fp32)
        table_raw = features[0:RP, 1].rearrange("p c f -> p (c f)").rearrange("p (o k d) -> p o k d", o=NO, k=CH)
        denseT = sb("denseT", [P, 2, SB], fp32)
        grams = sb("grams", [P, F, QUADS], fp32)
        gramsT = sb("gramsT", [P, F, FP], fp32)
        z = sb("z", [P, PAIRS], fp32)
        zT = sb("zT", [ZK, ZC, SB], fp32)
        h1 = sb("h1", [P, N1 // P, SB], fp32)
        h2 = sb("h2", [P, N2 // P, SB], fp32)
        y = sb("y", [P, TILES], fp32)
        w1z = sb("w1z", [ZK, ZC, N1], fp32)
        w1d = sb("w1d", [P, N1], fp32)
        w2_sb = sb("w2_sb", [P, N1 // P, N2], fp32)
        w3_sb = sb("w3_sb", [P, N2 // P], fp32)
        b1_sb = sb("b1_sb", [P, N1 // P], fp32)
        b2_sb = sb("b2_sb", [P, N2 // P], fp32)

        fillp = [pb(f"fillp{i}", [P, 512], fp32) for i in range(2)]
        gramp = [pb(f"gramp{i}", [P, 2, 512], fp32) for i in range(2)]
        mlpp = pb("mlpp", [P, 2, 512], fp32)
        idsp = mlpp[0:NO, :, :].rearrange("p b n -> p (b n)").bitcast(fp16)

        ids_loaded = sem("ids_loaded")
        gather_ids_loaded = [sem(f"gather_ids_loaded{i}") for i in range(2)]
        table_loaded = [sem(f"table_loaded{k}") for k in range(NO)]
        weights_loaded = sem("weights_loaded")
        rows_gathered = [sem(f"rows_gathered{i}") for i in range(2)]
        dense_loaded = [sem(f"dense_loaded{i}") for i in range(2)]
        gather_begun = sem("gather_begun")
        out_stored = sem("out_stored")
        zeroed = sem("zeroed")
        ident_made = sem("ident_made")
        ident16_made = sem("ident16_made")
        pick_made = sem("pick_made")
        ids_cast = sem("ids_cast")
        ids_transposed = sem("ids_transposed")
        ids_ready = sem("ids_ready")
        hi_ready = sem("hi_ready")
        lo_ready = sem("lo_ready")
        pads_zeroed = sem("pads_zeroed")
        onehot_built = sem("onehot_built")
        bank_filled = [sem(f"bank_filled{i}") for i in range(2)]
        bank_drained = [sem(f"bank_drained{i}") for i in range(2)]
        gram_filled = sem("gram_filled")
        gram_drained = [sem("gram_drained_act"), sem("gram_drained_dve")]
        gram_turned = sem("gram_turned")
        z_packed = sem("z_packed")
        h1_filled = sem("h1_filled")
        h1_ready = [sem("h1_ready_act"), sem("h1_ready_dve")]
        h2_filled = sem("h2_filled")
        h2_ready = sem("h2_ready")
        y_filled = sem("y_filled")
        y_ready = sem("y_ready")

        block = ctx.enter_context(nc.Block())

        def wait_filled(eng, s, name):
            bank, count = fill_of(s, name)
            eng.wait_ge(bank_filled[bank], count)
            return bank

        def wait_drained(eng, s, name):
            bank, count = fill_of(s, name)
            eng.wait_ge(bank_drained[bank], count)

        def run_of(fs):
            step = fs[1] - fs[0]
            return slice(fs[0], fs[-1] + 1, step)

        dense_v = dense.rearrange("(p t) d -> p t d", t=TILES)

        @block.sync
        def _(sp):
            ids_v = ids.rearrange("(p t) f -> p t f", t=TILES)

            def load_ids(t, tile):
                sp.dma_start(gather_ids[:, t, :], ids_v[:, tile, :]).then_inc(gather_ids_loaded[t], 16)

            load_ids(0, 0)
            sp.dma_start(ids_raw[:, :, :], ids_v).then_inc(ids_loaded, 16)
            load_ids(1, 1)

            def load_dense(t, tile):
                sp.dma_start(rows[:, t, NG, :], dense_v[:, tile, :]).then_inc(dense_loaded[t], 16)

            for k, f in enumerate(ONEHOT):
                sp.dma_start(table_raw[:, k], tables[f].rearrange("(p k) d -> p k d", k=CH)).then_inc(table_loaded[k], 16)
                if k < 2:
                    load_dense(k, k)
            sp.dma_start(w1z[:, :, :], w1[0:PAIRS, :].rearrange("(c p) n -> p c n", c=ZC)).then_inc(weights_loaded, 16)
            sp.dma_start(w1d[:, :], w1[PAIRS:PAIRS + D, :]).then_inc(weights_loaded, 16)
            sp.dma_start(w2_sb[:, :, :], w2.rearrange("(c p) n -> p c n", p=P)).then_inc(weights_loaded, 16)
            sp.dma_start(w3_sb[:, :], w3.rearrange("(c p) o -> p (c o)", p=P),
                         allow_slow_non_contiguous=True).then_inc(weights_loaded, 16)
            sp.dma_start(b1_sb[:, :], b1.rearrange("(c p) -> p c", p=P),
                         allow_slow_non_contiguous=True).then_inc(weights_loaded, 16)
            sp.dma_start(b2_sb[:, :], b2.rearrange("(c p) -> p c", p=P),
                         allow_slow_non_contiguous=True).then_inc(weights_loaded, 16)
            with sp.Fori(1, SUPER) as s:
                for t in range(2):
                    sp.wait_ge(gram_filled, (s - 1) * 8 + 4 * t + 1)
                    load_ids(t, bass.ds(s * 2 + t, 1))
                    load_dense(t, bass.ds(s * 2 + t, 1))
            sp.wait_ge(y_ready, SUPER)
            sp.dma_start(out.rearrange("(p t) o -> p (t o)", t=TILES), y[:, :]).then_inc(out_stored, 16)
            sp.wait_ge(out_stored, 16)

        WEIGHTS = 6 * 16

        @block.gpsimd
        def _(pool):
            pool.wait_ge(zeroed, 1)
            pool.affine_select(out=ident[:, :], in_=ident[:, :], compare_op=ALU.not_equal, fill=1.0,
                               base=0, pattern=[[-1, P]], channel_multiplier=1).then_inc(ident_made, 1)
            pool.iota(pick[:, :, :], [[0, NO], [-CH, P]], base=0, channel_multiplier=0,
                      allow_small_or_imprecise_dtypes=True).then_inc(pick_made, 1)
            pool.wait_ge(pick_made, 1)
            pool.affine_select(out=pick[:, :, :], in_=pick[:, :, :], compare_op=ALU.is_ge, fill=0.0,
                               base=-NO, pattern=[[0, NO], [0, P]], channel_multiplier=1).then_inc(pick_made, 1)
            pool.wait_ge(pick_made, 2)
            pool.affine_select(out=pick[:, :, :], in_=pick[:, :, :], compare_op=ALU.is_ge, fill=0.0,
                               base=NO, pattern=[[0, NO], [0, P]], channel_multiplier=-1).then_inc(pick_made, 1)
            pool.wait_ge(pick_made, 3)
            pool.affine_select(out=pick[:, :, :], in_=pick[:, :, :], compare_op=ALU.not_equal, fill=1.0,
                               base=0, pattern=[[-1, NO], [0, P]], channel_multiplier=1).then_inc(pick_made, 1)

            def gather(t, s):
                pool.wait_ge(gather_ids_loaded[t], (s + 1) * 16)
                pool.sem_inc(gather_begun, 1)
                for slot, f in enumerate(GATHERED):
                    pool.indirect_dma_start(
                        rows[:, t, slot, :], None, tables[f],
                        bass.IndirectOffsetOnAxis(ap=gather_ids[:, t, f:f + 1], axis=0)).then_inc(rows_gathered[t], 16)

            for t in range(2):
                gather(t, 0)
            with pool.Fori(1, SUPER) as s:
                for t in range(2):
                    pool.wait_ge(gram_filled, (s - 1) * 8 + 4 * t + 1)
                    gather(t, s)

        @block.tensor
        def _(pe):
            def open_fill(s, name):
                bank, count = fill_of(s, name)
                if not isinstance(count, int) or count > 1:
                    pe.wait_ge(bank_drained[bank], count - 1)
                return bank

            def ids_fill(it, s, p):
                bank = open_fill(it, ("ids", p))
                for j in range(2):
                    last = pe.matmul(fillp[bank][:, j * SB:(j + 1) * SB], pick[:, 2 * p + j, :],
                                     ids_rows[:, bass.ds(s * SB, SB)], start=True, stop=True)
                last.then_inc(bank_filled[bank], 1)

            def lookup_fill(it, s, p):
                bank = open_fill(it, ("lookup", p))
                for j in range(2):
                    k = 2 * p + j
                    pe.wait_ge(onehot_built, s * NO + k + 1)
                    if isinstance(it, int) and it < 0:
                        pe.wait_ge(hi_ready, k + 1)
                        pe.wait_ge(lo_ready, k + 1)
                    for half, table in enumerate((table_hi, table_lo)):
                        for c in range(CH):
                            last = pe.matmul(fillp[bank][:, j * SB:(j + 1) * SB], table[:, k, c, :],
                                             onehot[:, j, c, :], start=(half == 0 and c == 0),
                                             stop=(half == 1 and c == CH - 1))
                last.then_inc(bank_filled[bank], 1)

            def rows_fill(s, t, g):
                bank = open_fill(s, ("rows", t, g))
                if g == 0:
                    pe.wait_ge(rows_gathered[t], (s + 1) * (16 * NG))
                if g == len(GROUPS) - 1:
                    pe.wait_ge(dense_loaded[t], (s + 1) * 16)
                slot = sum(len(x) for x in GROUPS[:g])
                for j in range(len(GROUPS[g])):
                    last = pe.transpose(fillp[bank][:, j * D:(j + 1) * D], rows[:, t, slot + j, :], ident[:, :])
                last.then_inc(bank_filled[bank], 1)

            def z_fill(it, s, t):
                bank = open_fill(it, ("z", t))
                pe.wait_ge(z_packed, s * 2 + t + 1)
                for c in range(ZC):
                    last = pe.transpose(fillp[bank][0:ZK, c * P:(c + 1) * P], z[:, c * ZK:(c + 1) * ZK], ident[:, :])
                last.then_inc(bank_filled[bank], 1)

            def gram(s, parity, t):
                for name in ROWT[t][-2:]:
                    wait_drained(pe, s, name)
                for g in range(4):
                    pair = g % 2
                    if not (isinstance(s, int) and s == 0 and t == 0 and g < 2):
                        pe.wait_ge(gram_drained[pair], s * 4 + 2 * t + g // 2)
                    for q in range(8):
                        quad = features[:, parity, t * P + 4 * (8 * g + q):t * P + 4 * (8 * g + q + 1), :]
                        last = pe.matmul(gramp[pair][:, q // 4, (q % 4) * 4 * F:(q % 4 + 1) * 4 * F],
                                         quad.rearrange("d j f -> d (j f)"), quad[:, :, 0:F], start=True, stop=True)
                    last.then_inc(gram_filled, 1)

            def layer1(it, m, parity):
                for half in range(2):
                    if half == 0:
                        wait_drained(pe, it, ("z", 1))
                    for j in range(2):
                        n = 2 * half + j
                        o = mlpp[:, half, j * SB:(j + 1) * SB]
                        pe.matmul(o, w1d[:, n * P:(n + 1) * P], denseT[:, parity, :], start=True, stop=False)
                        for c in range(ZC):
                            last = pe.matmul(o, w1z[:, c, n * P:(n + 1) * P], zT[:, c, :], start=False, stop=(c == ZC - 1))
                    last.then_inc(h1_filled, 1)

            def layer2(m):
                pe.wait_ge(h1_ready[0], m + 1)
                pe.wait_ge(h1_ready[1], m + 1)
                for n in range(N2 // P):
                    for c in range(N1 // P):
                        last = pe.matmul(mlpp[:, 0, n * SB:(n + 1) * SB], w2_sb[:, c, n * P:(n + 1) * P],
                                         h1[:, c, :], start=(c == 0), stop=(c == N1 // P - 1))
                last.then_inc(h2_filled, 1)

            def layer3(m):
                pe.wait_ge(h2_ready, m + 1)
                for t in range(2):
                    for c in range(N2 // P):
                        last = pe.matmul(mlpp[:, 1, t:t + 1], h2[:, c, t * P:(t + 1) * P], w3_sb[:, c:c + 1],
                                         start=(c == 0), stop=(c == N2 // P - 1))
                last.then_inc(y_filled, 1)

            def next_layer1(m):
                pe.wait_ge(y_ready, m + 1)

            def superblock(s, parity):
                first = isinstance(s, int) and s == 0
                ahead = not (isinstance(s, int) and s == SUPER - 1)
                for g in range(len(GROUPS)):
                    rows_fill(s, 0, g)
                if not first:
                    z_fill(s, s - 1, 1)
                if ahead:
                    ids_fill(s, s + 1, 0)
                    ids_fill(s, s + 1, 1)
                if not first:
                    layer1(s, s - 1, 1 - parity)
                gram(s, parity, 0)
                if ahead:
                    lookup_fill(s, s + 1, 0)
                if not first:
                    layer2(s - 1)
                if ahead:
                    lookup_fill(s, s + 1, 1)
                if not first:
                    layer3(s - 1)
                if ahead:
                    ids_fill(s, s + 1, 2)
                    ids_fill(s, s + 1, 3)
                z_fill(s, s, 0)
                for g in range(len(GROUPS)):
                    rows_fill(s, 1, g)
                if ahead:
                    lookup_fill(s, s + 1, 2)
                if not first:
                    next_layer1(s - 1)
                gram(s, parity, 1)
                if ahead:
                    lookup_fill(s, s + 1, 3)

            pe.wait_ge(ident16_made, 1)
            pe.wait_ge(ids_cast, 1)
            for t in range(TILES):
                last = pe.transpose(idsp[:, t * P:(t + 1) * P], ids_half[:, t, :], ident16[:, :])
            last.then_inc(ids_transposed, 1)
            pe.wait_ge(ids_ready, 1)
            pe.wait_ge(pick_made, 4)
            pe.wait_ge(ident_made, 1)
            for kind, p in AHEAD:
                (ids_fill if kind == "ids" else lookup_fill)(-1, 0, p)
            pe.wait_ge(pads_zeroed, 2)
            superblock(0, 0)
            pe.wait_ge(weights_loaded, WEIGHTS)
            with pe.Fori(0, SUPER // 2 - 1) as i:
                superblock(i * 2 + 1, 1)
                superblock(i * 2 + 2, 0)
            superblock(SUPER - 1, 1)
            z_fill(SUPER, SUPER - 1, 1)
            layer1(SUPER, SUPER - 1, 1)
            layer2(SUPER - 1)
            layer3(SUPER - 1)

        def copy_on(eng):
            if eng is nc.scalar:
                return lambda o, i: nc.scalar.activation(o, i, ACT.Copy)
            return lambda o, i: nc.vector.tensor_copy(o, i)

        def drain_rows(wait, copy, s, parity, t, g):
            bank = wait_filled(wait, s, ("rows", t, g))
            dst = features[:, parity, t * P:(t + 1) * P, :].rearrange("d (q j) f -> d f j q", j=4)
            src = fillp[bank][:, :].rearrange("d (f j q) -> d f j q", j=4, q=QUADS)
            fs = GROUPS[g]
            if fs[-1] == NF:
                copy(dst[:, fs[0]], src[:, 0])
                copy(dst[:, fs[1]:fs[2] + 1], src[:, 1:3])
                last = copy(denseT[:, parity, t * P:(t + 1) * P], fillp[bank][:, 2 * P:3 * P])
            else:
                last = copy(dst[:, run_of(fs)], src)
            last.then_inc(bank_drained[bank], 1)

        def drain_gram(wait, copy, s, t, g):
            pair = g % 2
            wait.wait_ge(gram_filled, s * 8 + 4 * t + g + 1)
            for j in range(4):
                src = gramp[pair][32 * j:32 * j + 32, :, 0:16 * F].rearrange("f b (q g) -> f g b q", q=4)
                dst = grams[32 * j:32 * j + 32, :, 8 * g:8 * g + 8].rearrange("f g (b q) -> f g b q", b=2)
                last = copy(dst, src[:, j * F:(j + 1) * F])
            last.then_inc(gram_drained[pair], 1)

        @block.scalar
        def _(act):
            copy = copy_on(nc.scalar)

            def drain_ids(it, p):
                bank = wait_filled(act, it, ("ids", p))
                copy(offsets[:, p % 2].rearrange("p j c -> p (j c)"), fillp[bank][:, :]).then_inc(bank_drained[bank], 1)

            def drain_lookup(it, parity, p):
                bank = wait_filled(act, it, ("lookup", p))
                dst = features[:, parity, :, :].rearrange("d c f -> d f c")[:, run_of(ONEHOT[2 * p:2 * p + 2])]
                copy(dst, fillp[bank][:, :].rearrange("d (f c) -> d f c", f=2)).then_inc(bank_drained[bank], 1)

            def drain_z(it, t):
                bank = wait_filled(act, it, ("z", t))
                copy(zT[:, :, t * P:(t + 1) * P],
                     fillp[bank][0:ZK, 0:ZC * P].rearrange("k (c n) -> k c n", c=ZC)).then_inc(bank_drained[bank], 1)

            def relu1(m):
                act.wait_ge(h1_filled, m * 2 + 1)
                for n in range(2):
                    last = act.activation(h1[:, n, :], mlpp[:, 0, n * SB:(n + 1) * SB], ACT.Relu, bias=b1_sb[:, n:n + 1])
                last.then_inc(h1_ready[0], 1)

            def relu2(m):
                act.wait_ge(h2_filled, m + 1)
                for n in range(2):
                    last = act.activation(h2[:, n, :], mlpp[:, 0, n * SB:(n + 1) * SB], ACT.Relu, bias=b2_sb[:, n:n + 1])
                last.then_inc(h2_ready, 1)

            def grams_half(s, t):
                if not (isinstance(s, int) and s == 0 and t == 0):
                    act.wait_ge(gram_turned, s * 2 + t)
                for g in (0, 2):
                    drain_gram(act, copy, s, t, g)

            def superblock(s, parity):
                first = isinstance(s, int) and s == 0
                ahead = not (isinstance(s, int) and s == SUPER - 1)
                for g in (0, 2, 4):
                    drain_rows(act, copy, s, parity, 0, g)
                if not first:
                    drain_z(s, 1)
                if ahead:
                    drain_ids(s, 0)
                    drain_ids(s, 1)
                if not first:
                    relu1(s - 1)
                grams_half(s, 0)
                if ahead:
                    drain_lookup(s, 1 - parity, 0)
                if not first:
                    relu2(s - 1)
                if ahead:
                    drain_lookup(s, 1 - parity, 1)
                    drain_ids(s, 2)
                    drain_ids(s, 3)
                drain_z(s, 0)
                for g in (0, 2, 4):
                    drain_rows(act, copy, s, parity, 1, g)
                if ahead:
                    drain_lookup(s, 1 - parity, 2)
                grams_half(s, 1)
                if ahead:
                    drain_lookup(s, 1 - parity, 3)

            act.wait_ge(ids_transposed, 1)
            copy(ids_rows[0:NO, :].rearrange("k (t q j) -> k t j q", j=4, q=QUADS),
                 idsp.rearrange("k (t j q) -> k t j q", j=4, q=QUADS)).then_inc(ids_ready, 1)
            for p in range(2):
                drain_ids(-1, p)
            for k in range(NO):
                act.wait_ge(table_loaded[k], 16)
                copy(table_hi[:, k], table_raw[:, k]).then_inc(hi_ready, 1)
                if k == 4:
                    drain_lookup(-1, 0, 0)
            drain_lookup(-1, 0, 1)
            drain_ids(-1, 2)
            drain_ids(-1, 3)
            drain_lookup(-1, 0, 2)
            drain_lookup(-1, 0, 3)
            act.wait_ge(lo_ready, NO)
            superblock(0, 0)
            with act.Fori(0, SUPER // 2 - 1) as i:
                superblock(i * 2 + 1, 1)
                superblock(i * 2 + 2, 0)
            superblock(SUPER - 1, 1)
            drain_z(SUPER, 1)
            relu1(SUPER - 1)
            relu2(SUPER - 1)

        @block.vector
        def _(dve):
            copy = copy_on(nc.vector)

            def build(it, previous, p, j):
                if j == 0:
                    wait_drained(dve, it, ("ids", p))
                    if previous is not None:
                        wait_filled(dve, *previous)
                for c in range(CH):
                    last = dve.tensor_scalar(onehot[:, j, c, :], offsets[0:RP, p % 2, j, :], float(c), None, ALU.is_equal)
                last.then_inc(onehot_built, 1)

            def relu1(m):
                dve.wait_ge(h1_filled, m * 2 + 2)
                for n in range(2):
                    last = dve.tensor_scalar(h1[:, 2 + n, :], mlpp[:, 1, n * SB:(n + 1) * SB],
                                             b1_sb[:, 2 + n:3 + n], 0.0, ALU.add, ALU.max)
                last.then_inc(h1_ready[1], 1)

            def pack(s, t):
                dve.wait_ge(gram_drained[0], s * 4 + 2 * t + 2)
                dve.wait_ge(gram_drained[1], s * 4 + 2 * t + 2)
                if not (isinstance(s, int) and s == 0 and t == 0):
                    dve.wait_ge(z_packed, s * 2 + t)
                dve.transpose(gramsT[:, :, :].rearrange("p g f -> p (g f)"),
                              grams[:, :, :].rearrange("p g q -> p (g q)")).then_inc(gram_turned, 1)
                dve.wait_ge(gram_turned, s * 2 + t + 1)
                if t == 1:
                    wait_filled(dve, s, ("z", 0))
                elif not (isinstance(s, int) and s == 0):
                    wait_filled(dve, s, ("z", 1))
                at = 0
                for i in range(F - 1):
                    n = F - 1 - i
                    last = dve.tensor_copy(z[:, at:at + n], gramsT[:, i, i + 1:F])
                    at += n
                last.then_inc(z_packed, 1)

            def y_copy(m):
                dve.wait_ge(y_filled, m + 1)
                dve.tensor_copy(y[:, bass.ds(m * 2, 2)], mlpp[:, 1, 0:2]).then_inc(y_ready, 1)

            def superblock(s, parity):
                first = isinstance(s, int) and s == 0
                ahead = not (isinstance(s, int) and s == SUPER - 1)
                for g in (1, 3):
                    drain_rows(dve, copy, s, parity, 0, g)
                if ahead:
                    previous = (-1 if first else s - 1, ("lookup", NP - 1))
                    build(s, previous, 0, 0)
                    build(s, None, 0, 1)
                if not first:
                    relu1(s - 1)
                drain_gram(dve, copy, s, 0, 1)
                drain_gram(dve, copy, s, 0, 3)
                pack(s, 0)
                if ahead:
                    build(s, (s, ("lookup", 0)), 1, 0)
                    build(s, None, 1, 1)
                if not first:
                    y_copy(s - 1)
                if ahead:
                    build(s, (s, ("lookup", 1)), 2, 0)
                    build(s, None, 2, 1)
                for g in (1, 3):
                    drain_rows(dve, copy, s, parity, 1, g)
                drain_gram(dve, copy, s, 1, 1)
                if ahead:
                    build(s, (s, ("lookup", 2)), 3, 0)
                drain_gram(dve, copy, s, 1, 3)
                if ahead:
                    build(s, None, 3, 1)
                pack(s, 1)

            dve.memset(ident[:, :], 0.0).then_inc(zeroed, 1)
            dve.memset(ids_rows[:, :], 1.0).then_inc(zeroed, 1)
            dve.memset(features[:, 0, :, F:FP], 0.0).then_inc(pads_zeroed, 1)
            dve.wait_ge(ident_made, 1)
            dve.tensor_copy(ident16[:, :], ident[:, :]).then_inc(ident16_made, 1)
            dve.wait_ge(ids_loaded, 16)
            for k, f in enumerate(ONEHOT):
                last = dve.tensor_copy(ids_half[:, :, k], ids_raw[:, :, f])
            last.then_inc(ids_cast, 1)

            def split(k):
                dve.wait_ge(hi_ready, k + 1)
                dve.tensor_tensor(table_lo[:, k], table_raw[:, k], table_hi[:, k], ALU.subtract).then_inc(lo_ready, 1)

            for p in range(NP):
                previous = (-1, ("lookup", p - 1)) if p else None
                build(-1, previous, p, 0)
                split(2 * p)
                build(-1, None, p, 1)
                split(2 * p + 1)
            dve.wait_ge(lo_ready, NO)
            dve.memset(features[:, 1, :, F:FP], 0.0).then_inc(pads_zeroed, 1)
            superblock(0, 0)
            with dve.Fori(0, SUPER // 2 - 1) as i:
                superblock(i * 2 + 1, 1)
                superblock(i * 2 + 2, 0)
            superblock(SUPER - 1, 1)
            relu1(SUPER - 1)
            y_copy(SUPER - 1)


_TABLES = [f"tbl_{i}" for i in range(26)]
_INS = ["r_dense_x", "ids"] + _TABLES + ["W_top1", "b_top1", "W_top2", "b_top2", "W_top3"]


def kernel(**inputs):
    import numpy as _np
    import concourse.bacc as _bacc
    from concourse import mybir as _mybir
    from concourse.bass_utils import run_bass_kernel_spmd as _run

    nc = _bacc.Bacc("TRN2", target_bir_lowering=False, num_devices=1)
    arrays, args = {}, {}
    for name in _INS:
        a = _np.ascontiguousarray(inputs[name])
        arrays[f"in_{name}"] = a
        args[name] = nc.dram_tensor(f"in_{name}", a.shape, _mybir.dt.from_np(a.dtype), kind="ExternalInput").ap()
    out = nc.dram_tensor("out_y", (arrays["in_r_dense_x"].shape[0], 1), _mybir.dt.float32, kind="ExternalOutput").ap()
    dlrm_tower(nc, args["r_dense_x"], args["ids"], [args[n] for n in _TABLES],
               args["W_top1"], args["b_top1"], args["W_top2"], args["b_top2"], args["W_top3"], out)
    r = _run(nc, [arrays], core_ids=[0])
    return r.results[0]["out_y"]
```

```python
import concourse.bass as bass
from concourse import mybir
from contextlib import ExitStack


def dlrm_tower(nc, dense, ids, tables, w1, b1, w2, b2, w3, out):
    fp32, f32r = mybir.dt.float32, mybir.dt.float32r
    fp16, i32 = mybir.dt.float16, mybir.dt.int32
    ALU = mybir.AluOpType
    ACT = mybir.ActivationFunctionType

    P = 128
    B, D = dense.shape
    NF = len(tables)
    F = NF + 1
    FP = 32
    TILES = B // P
    SUPER = TILES // 2
    SB = 2 * P
    N1, N2 = w1.shape[1], w2.shape[1]
    PAIRS = F * (F - 1) // 2
    ZC = 3
    ZK = PAIRS // ZC
    QUADS = P // 4
    FG = F - 1

    LOOKUPS = [[1, 2], [5, 7], [8], [10, 11]]
    ONEHOT = [f for group in LOOKUPS for f in group]
    GROUPS = [[0, 3, 6, 9], [12, 13, 14, 15], [16, 17, 18, 19], [20, 21, 22, 23], [4, 24, 25, NF]]
    SLOTS = [f for group in GROUPS for f in group]
    GATHERED = SLOTS[:-1]
    NG, NO = len(GATHERED), len(ONEHOT)
    ROWS = tables[ONEHOT[0]].shape[0]
    CH = 8
    RP = ROWS // CH
    NL = len(LOOKUPS)
    AT = [sum(len(x) for x in LOOKUPS[:g]) for g in range(NL)]
    HOTS = 3
    GP = 2 * P // 32
    assert sorted(ONEHOT + SLOTS) == list(range(F)) and all(tables[f].shape[0] == ROWS for f in ONEHOT)

    def numbered(start, names):
        return {name: ((start + n) % 2, (start + n) // 2 + 1) for n, name in enumerate(names)}

    ID = [("ids", g) for g in range(NL)]
    ROWT = [[("rows", t, g) for g in range(len(GROUPS))] for t in range(2)]
    ORDER = ROWT[0][:2] + [("z", 1)] + ROWT[0][2:] + ID + [("z", 0)] + ROWT[1]
    AHEAD = ID
    PER = len(ORDER)
    BEFORE = numbered(0, AHEAD)
    first_order = [x for x in ORDER if x != ("z", 1)]
    last_order = [x for x in ORDER if x not in AHEAD]
    n1 = len(AHEAD) + len(first_order)
    FIRST = numbered(len(AHEAD), first_order)
    STEADY = numbered(n1, ORDER)
    LAST = numbered(n1 + PER * (SUPER - 2), last_order)
    AFTER = numbered(n1 + PER * (SUPER - 2) + len(last_order), [("z", 1)])
    assert PER % 2 == 0

    def fill_of(s, name):
        if isinstance(s, int):
            if s < 0:
                return BEFORE[name]
            if s == 0:
                return FIRST[name]
            if s == SUPER - 1:
                return LAST[name]
            if s == SUPER:
                return AFTER[name]
        bank, count = STEADY[name]
        return bank, (s - 1) * (PER // 2) + count

    ctx = ExitStack()
    with ctx:
        def sb(name, shape, dt):
            return ctx.enter_context(nc.sbuf_tensor(name, shape, dt))

        def pb(name, shape, dt):
            return ctx.enter_context(nc.psum_tensor(name, shape, dt))

        def sem(name):
            return ctx.enter_context(nc.semaphore(name))

        gather_ids = sb("gather_ids", [P, 2, NF], i32)
        ids_raw = sb("ids_raw", [P, TILES, NF], i32)
        ids_half = sb("ids_half", [P, TILES, NO], fp16)
        ids_rows = sb("ids_rows", [P, B], fp16)
        pick = sb("pick", [P, NO, P], fp16)
        minus_row = sb("minus_row", [P, 1], fp32)
        ident = sb("ident", [P, P], fp32)
        ident16 = sb("ident16", [P, P], fp16)
        table_hi = sb("table_hi", [RP, NO, CH, D], f32r)
        table_lo = sb("table_lo", [RP, NO, CH, D], f32r)
        ids_all = sb("ids_all", [P, NL, 2, SB], fp16)
        onehot = sb("onehot", [RP, HOTS, CH, SB], f32r)
        rows = sb("rows", [P, 2, NG + 1, D], fp32)
        features = sb("features", [P, 2, SB, FP], fp32)
        table_raw = features[0:RP, 1].rearrange("p c f -> p (c f)")[:, 0:NO * CH * D].rearrange("p (o k d) -> p o k d", o=NO, k=CH)
        denseT = sb("denseT", [P, 2, SB], fp32)
        grams = sb("grams", [P, FG, QUADS], fp32)
        gramsT = sb("gramsT", [P, FG, FP], fp32)
        z = sb("z", [P, PAIRS], fp32)
        zT = sb("zT", [ZK, ZC, SB], fp32)
        h1 = sb("h1", [P, N1 // P, SB], fp32)
        h2 = sb("h2", [P, N2 // P, SB], fp32)
        y = sb("y", [P, TILES], fp32)
        w1z = sb("w1z", [ZK, ZC, N1], fp32)
        w1d = sb("w1d", [P, N1], fp32)
        w2_sb = sb("w2_sb", [P, N1 // P, N2], fp32)
        w3_sb = sb("w3_sb", [P, N2 // P], fp32)
        b1_sb = sb("b1_sb", [P, N1 // P], fp32)
        b2_sb = sb("b2_sb", [P, N2 // P], fp32)

        fillp = [pb(f"fillp{i}", [P, 512], fp32) for i in range(2)]
        lookp = pb("lookp", [P, 512], fp32)
        gramp = [pb(f"gramp{i}", [P, 512], fp32) for i in range(3)]
        mlpp = pb("mlpp", [P, 2, 512], fp32)
        idsp = mlpp[0:NO, :, :].rearrange("p b n -> p (b n)").bitcast(fp16)

        ids_loaded = sem("ids_loaded")
        gather_ids_loaded = [sem(f"gather_ids_loaded{i}") for i in range(2)]
        table_loaded = [sem(f"table_loaded{k}") for k in range(NO)]
        weights_loaded = sem("weights_loaded")
        rows_gathered = [sem(f"rows_gathered{i}") for i in range(2)]
        dense_loaded = [sem(f"dense_loaded{i}") for i in range(2)]
        gather_begun = sem("gather_begun")
        out_stored = sem("out_stored")
        zeroed = sem("zeroed")
        ident_made = sem("ident_made")
        ident16_made = sem("ident16_made")
        pick_made = sem("pick_made")
        ids_cast = sem("ids_cast")
        ids_transposed = sem("ids_transposed")
        ids_ready = sem("ids_ready")
        hi_ready = sem("hi_ready")
        lo_ready = sem("lo_ready")
        pads_zeroed = sem("pads_zeroed")
        onehot_built = sem("onehot_built")
        looked_up = sem("looked_up")
        lookup_drained = sem("lookup_drained")
        rows_numbered = sem("rows_numbered")
        bank_filled = [sem(f"bank_filled{i}") for i in range(2)]
        bank_drained = [sem(f"bank_drained{i}") for i in range(2)]
        gram_filled = sem("gram_filled")
        gram_drained = sem("gram_drained")
        gram_turned = sem("gram_turned")
        z_packed = sem("z_packed")
        h1_filled = sem("h1_filled")
        h1_ready = [sem("h1_ready_act"), sem("h1_ready_dve")]
        h2_filled = sem("h2_filled")
        h2_ready = sem("h2_ready")
        y_filled = sem("y_filled")
        y_ready = sem("y_ready")

        block = ctx.enter_context(nc.Block())

        def wait_filled(eng, s, name):
            bank, count = fill_of(s, name)
            eng.wait_ge(bank_filled[bank], count)
            return bank

        def wait_drained(eng, s, name):
            bank, count = fill_of(s, name)
            eng.wait_ge(bank_drained[bank], count)

        def run_of(fs):
            return slice(fs[0], fs[-1] + 1, fs[1] - fs[0] if len(fs) > 1 else 1)

        dense_v = dense.rearrange("(p t) d -> p t d", t=TILES)

        @block.sync
        def _(sp):
            ids_v = ids.rearrange("(p t) f -> p t f", t=TILES)

            def load_ids(t, tile):
                sp.dma_start(gather_ids[:, t, :], ids_v[:, tile, :]).then_inc(gather_ids_loaded[t], 16)

            load_ids(0, 0)
            sp.dma_start(ids_raw[:, :, :], ids_v).then_inc(ids_loaded, 16)
            load_ids(1, 1)

            def load_dense(t, tile):
                sp.dma_start(rows[:, t, NG, :], dense_v[:, tile, :]).then_inc(dense_loaded[t], 16)

            for k, f in enumerate(ONEHOT):
                sp.dma_start(table_raw[:, k], tables[f].rearrange("(p k) d -> p k d", k=CH)).then_inc(table_loaded[k], 16)
                if k < 2:
                    load_dense(k, k)
            sp.dma_start(w1z[:, :, :], w1[0:PAIRS, :].rearrange("(c p) n -> p c n", c=ZC)).then_inc(weights_loaded, 16)
            sp.dma_start(w1d[:, :], w1[PAIRS:PAIRS + D, :]).then_inc(weights_loaded, 16)
            sp.dma_start(w2_sb[:, :, :], w2.rearrange("(c p) n -> p c n", p=P)).then_inc(weights_loaded, 16)
            sp.dma_start(w3_sb[:, :], w3.rearrange("(c p) o -> p (c o)", p=P),
                         allow_slow_non_contiguous=True).then_inc(weights_loaded, 16)
            sp.dma_start(b1_sb[:, :], b1.rearrange("(c p) -> p c", p=P),
                         allow_slow_non_contiguous=True).then_inc(weights_loaded, 16)
            sp.dma_start(b2_sb[:, :], b2.rearrange("(c p) -> p c", p=P),
                         allow_slow_non_contiguous=True).then_inc(weights_loaded, 16)
            with sp.Fori(1, SUPER) as s:
                for t in range(2):
                    sp.wait_ge(gram_filled, (s - 1) * (2 * GP) + GP * t + 1)
                    load_ids(t, bass.ds(s * 2 + t, 1))
                    load_dense(t, bass.ds(s * 2 + t, 1))
            sp.wait_ge(y_ready, SUPER)
            sp.dma_start(out.rearrange("(p t) o -> p (t o)", t=TILES), y[:, :]).then_inc(out_stored, 16)
            sp.wait_ge(out_stored, 16)

        WEIGHTS = 6 * 16

        @block.gpsimd
        def _(pool):
            pool.wait_ge(zeroed, 1)
            pool.affine_select(out=ident[:, :], in_=ident[:, :], compare_op=ALU.not_equal, fill=1.0,
                               base=0, pattern=[[-1, P]], channel_multiplier=1).then_inc(ident_made, 1)
            pool.iota(minus_row[:, :], [[0, 1]], base=0, channel_multiplier=-CH,
                      allow_small_or_imprecise_dtypes=True).then_inc(rows_numbered, 1)

            def gather(t, s):
                pool.wait_ge(gather_ids_loaded[t], (s + 1) * 16)
                pool.sem_inc(gather_begun, 1)
                for slot, f in enumerate(GATHERED):
                    pool.indirect_dma_start(
                        rows[:, t, slot, :], None, tables[f],
                        bass.IndirectOffsetOnAxis(ap=gather_ids[:, t, f:f + 1], axis=0)).then_inc(rows_gathered[t], 16)

            for t in range(2):
                gather(t, 0)
            with pool.Fori(1, SUPER) as s:
                for t in range(2):
                    pool.wait_ge(gram_filled, (s - 1) * (2 * GP) + GP * t + 1)
                    gather(t, s)

        @block.tensor
        def _(pe):
            def open_fill(s, name):
                bank, count = fill_of(s, name)
                if not isinstance(count, int) or count > 1:
                    pe.wait_ge(bank_drained[bank], count - 1)
                return bank

            def ids_fill(it, s, g):
                bank = open_fill(it, ("ids", g))
                for j in range(len(LOOKUPS[g])):
                    last = pe.matmul(fillp[bank][:, j * SB:(j + 1) * SB], pick[:, AT[g] + j, :],
                                     ids_rows[:, bass.ds(s * SB, SB)], start=True, stop=True)
                last.then_inc(bank_filled[bank], 1)

            def lookup_half(s, g, j, half):
                k = AT[g] + j
                if half == 0:
                    pe.wait_ge(onehot_built, s * NO + k + 1)
                    if isinstance(s, int) and s == 0:
                        pe.wait_ge(hi_ready, k + 1)
                elif isinstance(s, int) and s == 0:
                    pe.wait_ge(lo_ready, k + 1)
                if j == 0 and half == 0 and not (isinstance(s, int) and s == 0 and g == 0):
                    pe.wait_ge(lookup_drained, s * NL + g)
                table = (table_hi, table_lo)[half]
                for c in range(CH):
                    last = pe.matmul(lookp[:, j * SB:(j + 1) * SB], table[:, k, c, :], onehot[:, k % HOTS, c, :],
                                     start=(half == 0 and c == 0), stop=(half == 1 and c == CH - 1))
                if half == 1:
                    last.then_inc(looked_up, 1)

            def lookup(s, g):
                for j in range(len(LOOKUPS[g])):
                    for half in range(2):
                        lookup_half(s, g, j, half)

            def rows_fill(s, t, g):
                bank = open_fill(s, ("rows", t, g))
                if g == 0:
                    pe.wait_ge(rows_gathered[t], (s + 1) * (16 * NG))
                if g == len(GROUPS) - 1:
                    pe.wait_ge(dense_loaded[t], (s + 1) * 16)
                slot = sum(len(x) for x in GROUPS[:g])
                for j in range(len(GROUPS[g])):
                    last = pe.transpose(fillp[bank][:, j * D:(j + 1) * D], rows[:, t, slot + j, :], ident[:, :])
                last.then_inc(bank_filled[bank], 1)

            def z_fill(it, s, t):
                bank = open_fill(it, ("z", t))
                pe.wait_ge(z_packed, s * 2 + t + 1)
                for c in range(ZC):
                    last = pe.transpose(fillp[bank][0:ZK, c * P:(c + 1) * P], z[:, c * ZK:(c + 1) * ZK], ident[:, :])
                last.then_inc(bank_filled[bank], 1)

            def gram(s, parity, t):
                for name in ROWT[t][-2:]:
                    wait_drained(pe, s, name)
                pe.wait_ge(lookup_drained, s * NL + NL)
                for g in range(GP):
                    if g >= 3:
                        pe.wait_ge(gram_drained, (s * 2 + t) * GP + g - 2)
                    elif g == 0 and not (isinstance(s, int) and s == 0 and t == 0):
                        pe.wait_ge(gram_drained, (s * 2 + t) * GP)
                    for q in range(4):
                        quad = features[:, parity, t * P + 4 * (4 * g + q):t * P + 4 * (4 * g + q + 1), :]
                        last = pe.matmul(gramp[g % 3][:, q * 4 * FG:(q + 1) * 4 * FG],
                                         quad.rearrange("d j f -> d (j f)"), quad[:, :, 0:FG], start=True, stop=True)
                    last.then_inc(gram_filled, 1)

            def unit_chunk(n):
                return mlpp[:, n // 2, n % 2 * SB:(n % 2 + 1) * SB]

            def layer1_dense(parity, half):
                for n in (2 * half, 2 * half + 1):
                    pe.matmul(unit_chunk(n), w1d[:, n * P:(n + 1) * P], denseT[:, parity, :],
                              start=(n % 2 == 0), stop=False, skip_group_check=True)

            def layer1(it, n):
                if n == 0:
                    wait_drained(pe, it, ("z", 1))
                for c in range(ZC):
                    last = pe.matmul(unit_chunk(n), w1z[:, c, n * P:(n + 1) * P], zT[:, c, :],
                                     start=False, stop=(c == ZC - 1), skip_group_check=True)
                if n % 2 == 1:
                    last.then_inc(h1_filled, 1)

            def layer2(m, n):
                if n == 0:
                    pe.wait_ge(h1_ready[0], m + 1)
                    pe.wait_ge(h1_ready[1], m + 1)
                for c in range(N1 // P):
                    last = pe.matmul(mlpp[:, 0, n * SB:(n + 1) * SB], w2_sb[:, c, n * P:(n + 1) * P],
                                     h1[:, c, :], start=(c == 0), stop=(c == N1 // P - 1))
                if n == 1:
                    last.then_inc(h2_filled, 1)

            def layer3(m):
                pe.wait_ge(h2_ready, m + 1)
                for t in range(2):
                    for c in range(N2 // P):
                        last = pe.matmul(mlpp[:, 1, t:t + 1], h2[:, c, t * P:(t + 1) * P], w3_sb[:, c:c + 1],
                                         start=(c == 0), stop=(c == N2 // P - 1))
                last.then_inc(y_filled, 1)

            def next_layer1(m):
                pe.wait_ge(y_ready, m + 1)

            def superblock(s, parity):
                mlp = not (isinstance(s, int) and s == 0)
                ahead = not (isinstance(s, int) and s == SUPER - 1)
                rows_fill(s, 0, 0)
                rows_fill(s, 0, 1)
                if mlp:
                    layer1_dense(1 - parity, 0)
                    z_fill(s, s - 1, 1)
                rows_fill(s, 0, 2)
                if mlp:
                    layer1_dense(1 - parity, 1)
                    layer1(s, 0)
                rows_fill(s, 0, 3)
                rows_fill(s, 0, 4)
                if mlp:
                    layer1(s, 1)
                if ahead:
                    ids_fill(s, s + 1, 0)
                    ids_fill(s, s + 1, 1)
                if mlp:
                    layer1(s, 2)
                    layer1(s, 3)
                gram(s, parity, 0)
                if ahead:
                    lookup(s + 1, 0)
                if mlp:
                    layer2(s - 1, 0)
                if ahead:
                    ids_fill(s, s + 1, 2)
                    ids_fill(s, s + 1, 3)
                if mlp:
                    layer2(s - 1, 1)
                if ahead:
                    lookup(s + 1, 1)
                z_fill(s, s, 0)
                rows_fill(s, 1, 0)
                rows_fill(s, 1, 1)
                if ahead:
                    lookup_half(s + 1, 2, 0, 0)
                rows_fill(s, 1, 2)
                rows_fill(s, 1, 3)
                if ahead:
                    lookup_half(s + 1, 2, 0, 1)
                rows_fill(s, 1, 4)
                if mlp:
                    layer3(s - 1)
                gram(s, parity, 1)
                if mlp:
                    next_layer1(s - 1)
                if ahead:
                    lookup(s + 1, 3)

            pe.wait_ge(ident16_made, 1)
            pe.wait_ge(ids_cast, 1)
            for t in range(TILES):
                last = pe.transpose(idsp[:, t * P:(t + 1) * P], ids_half[:, t, :], ident16[:, :])
            last.then_inc(ids_transposed, 1)
            pe.wait_ge(ids_ready, 1)
            pe.wait_ge(pick_made, 1)
            pe.wait_ge(ident_made, 1)
            for g in range(NL):
                ids_fill(-1, 0, g)
            for g in range(NL):
                lookup(0, g)
            pe.wait_ge(pads_zeroed, 2)
            superblock(0, 0)
            pe.wait_ge(weights_loaded, WEIGHTS)
            with pe.Fori(0, SUPER // 2 - 1) as i:
                superblock(i * 2 + 1, 1)
                superblock(i * 2 + 2, 0)
            superblock(SUPER - 1, 1)
            layer1_dense(1, 0)
            layer1_dense(1, 1)
            z_fill(SUPER, SUPER - 1, 1)
            for n in range(N1 // P):
                layer1(SUPER, n)
            for n in range(N2 // P):
                layer2(SUPER - 1, n)
            layer3(SUPER - 1)

        @block.scalar
        def _(act):
            def copy(o, i):
                return act.activation(o, i, ACT.Copy)

            def drain_rows(s, parity, t, g):
                bank = wait_filled(act, s, ("rows", t, g))
                dst = features[:, parity, t * P:(t + 1) * P, :].rearrange("d (q j) f -> d f j q", j=4)
                src = fillp[bank][:, :].rearrange("d (f j q) -> d f j q", j=4, q=QUADS)
                fs = GROUPS[g]
                if fs[-1] == NF:
                    copy(dst[:, fs[0]], src[:, 0])
                    copy(dst[:, fs[1]:NF + 1], src[:, 1:])
                    last = copy(denseT[:, parity, t * P:(t + 1) * P], fillp[bank][:, (len(fs) - 1) * P:len(fs) * P])
                else:
                    last = copy(dst[:, run_of(fs)], src)
                last.then_inc(bank_drained[bank], 1)

            def drain_gram(s, t, g):
                act.wait_ge(gram_filled, s * (2 * GP) + GP * t + g + 1)
                for j in range(4):
                    src = gramp[g % 3][32 * j:32 * j + 32, 0:16 * FG].rearrange("f (q c) -> f c q", q=4)
                    last = copy(grams[32 * j:32 * j + 32, :, 4 * g:4 * g + 4], src[:, j * FG:(j + 1) * FG])
                last.then_inc(gram_drained, 1)

            def drain_ids(it, g):
                bank = wait_filled(act, it, ("ids", g))
                n = len(LOOKUPS[g]) * SB
                act.activation(ids_all[:, g].rearrange("p j c -> p (j c)")[:, 0:n], fillp[bank][:, 0:n], ACT.Identity,
                               bias=minus_row[:, :]).then_inc(bank_drained[bank], 1)

            def drain_lookup(s, parity, g):
                act.wait_ge(looked_up, s * NO + AT[g] + len(LOOKUPS[g]))
                dst = features[:, parity, :, :].rearrange("d c f -> d f c")[:, run_of(LOOKUPS[g])]
                n = len(LOOKUPS[g])
                copy(dst, lookp[:, 0:n * SB].rearrange("d (f c) -> d f c", f=n)).then_inc(lookup_drained, 1)

            def drain_z(it, t):
                bank = wait_filled(act, it, ("z", t))
                copy(zT[:, :, t * P:(t + 1) * P],
                     fillp[bank][0:ZK, 0:ZC * P].rearrange("k (c n) -> k c n", c=ZC)).then_inc(bank_drained[bank], 1)

            def relu1(m):
                act.wait_ge(h1_filled, m * 2 + 1)
                for n in range(2):
                    last = act.activation(h1[:, n, :], mlpp[:, 0, n * SB:(n + 1) * SB], ACT.Relu, bias=b1_sb[:, n:n + 1])
                last.then_inc(h1_ready[0], 1)

            def relu2(m):
                act.wait_ge(h2_filled, m + 1)
                for n in range(2):
                    last = act.activation(h2[:, n, :], mlpp[:, 0, n * SB:(n + 1) * SB], ACT.Relu, bias=b2_sb[:, n:n + 1])
                last.then_inc(h2_ready, 1)

            def drain_grams(s, t):
                if not (isinstance(s, int) and s == 0 and t == 0):
                    act.wait_ge(gram_turned, s * 2 + t)
                for g in range(GP):
                    drain_gram(s, t, g)

            def superblock(s, parity):
                mlp = not (isinstance(s, int) and s == 0)
                ahead = not (isinstance(s, int) and s == SUPER - 1)
                drain_rows(s, parity, 0, 0)
                drain_rows(s, parity, 0, 1)
                if mlp:
                    drain_z(s, 1)
                for g in (2, 3, 4):
                    drain_rows(s, parity, 0, g)
                if mlp:
                    relu1(s - 1)
                if ahead:
                    drain_ids(s, 0)
                    drain_ids(s, 1)
                drain_grams(s, 0)
                if ahead:
                    drain_lookup(s + 1, 1 - parity, 0)
                    drain_ids(s, 2)
                    drain_ids(s, 3)
                if mlp:
                    relu2(s - 1)
                if ahead:
                    drain_lookup(s + 1, 1 - parity, 1)
                drain_z(s, 0)
                for g in range(4):
                    drain_rows(s, parity, 1, g)
                if ahead:
                    drain_lookup(s + 1, 1 - parity, 2)
                drain_rows(s, parity, 1, 4)
                drain_grams(s, 1)
                if ahead:
                    drain_lookup(s + 1, 1 - parity, 3)

            act.wait_ge(rows_numbered, 1)
            act.wait_ge(ids_transposed, 1)
            copy(ids_rows[0:NO, :].rearrange("k (t q j) -> k t j q", j=4, q=QUADS),
                 idsp.rearrange("k (t j q) -> k t j q", j=4, q=QUADS)).then_inc(ids_ready, 1)
            for g in range(NL):
                drain_ids(-1, g)
            for k in range(NO):
                act.wait_ge(table_loaded[k], 16)
                copy(table_hi[:, k], table_raw[:, k]).then_inc(hi_ready, 1)
            for g in range(NL):
                drain_lookup(0, 0, g)
            act.wait_ge(lo_ready, NO)
            superblock(0, 0)
            with act.Fori(0, SUPER // 2 - 1) as i:
                superblock(i * 2 + 1, 1)
                superblock(i * 2 + 2, 0)
            superblock(SUPER - 1, 1)
            drain_z(SUPER, 1)
            relu1(SUPER - 1)
            relu2(SUPER - 1)

        @block.vector
        def _(dve):
            def build(it, s, k):
                g = max(x for x in range(NL) if AT[x] <= k)
                j = k - AT[g]
                if j == 0:
                    wait_drained(dve, it, ("ids", g))
                if k >= HOTS:
                    dve.wait_ge(looked_up, s * NO + k - HOTS + 1)
                elif k == 0 and not (isinstance(s, int) and s == 0):
                    dve.wait_ge(looked_up, s * NO)
                for c in range(CH):
                    last = dve.tensor_scalar(onehot[:, k % HOTS, c, :], ids_all[0:RP, g, j, :],
                                             float(c), None, ALU.is_equal)
                last.then_inc(onehot_built, 1)

            def relu1(m):
                dve.wait_ge(h1_filled, m * 2 + 2)
                for n in range(2):
                    last = dve.tensor_scalar(h1[:, 2 + n, :], mlpp[:, 1, n * SB:(n + 1) * SB],
                                             b1_sb[:, 2 + n:3 + n], 0.0, ALU.add, ALU.max)
                last.then_inc(h1_ready[1], 1)

            def pack(s, t):
                dve.wait_ge(gram_drained, (s * 2 + t + 1) * GP)
                if not (isinstance(s, int) and s == 0 and t == 0):
                    dve.wait_ge(z_packed, s * 2 + t)
                dve.transpose(gramsT[:, :, :].rearrange("p g f -> p (g f)"),
                              grams[:, :, :].rearrange("p g q -> p (g q)")).then_inc(gram_turned, 1)
                dve.wait_ge(gram_turned, s * 2 + t + 1)
                if t == 1:
                    wait_filled(dve, s, ("z", 0))
                elif not (isinstance(s, int) and s == 0):
                    wait_filled(dve, s, ("z", 1))
                at = 0
                for i in range(F - 1):
                    n = F - 1 - i
                    last = dve.tensor_copy(z[:, at:at + n], gramsT[:, i, i + 1:F])
                    at += n
                last.then_inc(z_packed, 1)

            def y_copy(m):
                dve.wait_ge(y_filled, m + 1)
                dve.tensor_copy(y[:, bass.ds(m * 2, 2)], mlpp[:, 1, 0:2]).then_inc(y_ready, 1)

            def superblock(s):
                mlp = not (isinstance(s, int) and s == 0)
                ahead = not (isinstance(s, int) and s == SUPER - 1)
                if ahead:
                    build(s, s + 1, 0)
                    build(s, s + 1, 1)
                if mlp:
                    relu1(s - 1)
                if ahead:
                    build(s, s + 1, 2)
                pack(s, 0)
                if ahead:
                    for k in (3, 4, 5):
                        build(s, s + 1, k)
                if mlp:
                    y_copy(s - 1)
                if ahead:
                    build(s, s + 1, 6)
                pack(s, 1)

            dve.memset(ident[:, :], 0.0).then_inc(zeroed, 1)
            dve.memset(ids_rows[:, :], 1.0).then_inc(zeroed, 1)
            dve.memset(features[:, 0, :, F:FP], 0.0).then_inc(pads_zeroed, 1)
            dve.wait_ge(ident_made, 1)
            dve.tensor_copy(ident16[:, :], ident[:, :]).then_inc(ident16_made, 1)
            dve.wait_ge(ident16_made, 1)
            dve.tensor_copy(pick[:, :, :], ident16[:, 0:NO].unsqueeze(2).to_broadcast([P, NO, P])).then_inc(pick_made, 1)
            dve.wait_ge(ids_loaded, 16)
            for k, f in enumerate(ONEHOT):
                last = dve.tensor_copy(ids_half[:, :, k], ids_raw[:, :, f])
            last.then_inc(ids_cast, 1)

            def split(k):
                dve.wait_ge(hi_ready, k + 1)
                dve.tensor_tensor(table_lo[:, k], table_raw[:, k], table_hi[:, k], ALU.subtract).then_inc(lo_ready, 1)

            for k in range(NO):
                build(-1, 0, k)
                split(k)
            dve.wait_ge(lo_ready, NO)
            dve.memset(features[:, 1, :, F:FP], 0.0).then_inc(pads_zeroed, 1)
            superblock(0)
            with dve.Fori(0, SUPER // 2 - 1) as i:
                superblock(i * 2 + 1)
                superblock(i * 2 + 2)
            superblock(SUPER - 1)
            relu1(SUPER - 1)
            y_copy(SUPER - 1)


_TABLES = [f"tbl_{i}" for i in range(26)]
_INS = ["r_dense_x", "ids"] + _TABLES + ["W_top1", "b_top1", "W_top2", "b_top2", "W_top3"]


def kernel(**inputs):
    import numpy as _np
    import concourse.bacc as _bacc
    from concourse import mybir as _mybir
    from concourse.bass_utils import run_bass_kernel_spmd as _run

    nc = _bacc.Bacc("TRN2", target_bir_lowering=False, num_devices=1)
    arrays, args = {}, {}
    for name in _INS:
        a = _np.ascontiguousarray(inputs[name])
        arrays[f"in_{name}"] = a
        args[name] = nc.dram_tensor(f"in_{name}", a.shape, _mybir.dt.from_np(a.dtype), kind="ExternalInput").ap()
    out = nc.dram_tensor("out_y", (arrays["in_r_dense_x"].shape[0], 1), _mybir.dt.float32, kind="ExternalOutput").ap()
    dlrm_tower(nc, args["r_dense_x"], args["ids"], [args[n] for n in _TABLES],
               args["W_top1"], args["b_top1"], args["W_top2"], args["b_top2"], args["W_top3"], out)
    r = _run(nc, [arrays], core_ids=[0])
    return r.results[0]["out_y"]
```

```python
import concourse.bass as bass
from concourse import mybir
from contextlib import ExitStack


def dlrm_tower(nc, dense, ids, tables, w1, b1, w2, b2, w3, out):
    fp32, f32r = mybir.dt.float32, mybir.dt.float32r
    fp16, i32 = mybir.dt.float16, mybir.dt.int32
    ALU = mybir.AluOpType
    ACT = mybir.ActivationFunctionType

    P = 128
    B, D = dense.shape
    NF = len(tables)
    F = NF + 1
    FP = 32
    TILES = B // P
    SUPER = TILES // 2
    SB = 2 * P
    N1, N2 = w1.shape[1], w2.shape[1]
    PAIRS = F * (F - 1) // 2
    ZC = 3
    ZK = PAIRS // ZC
    QUADS = P // 4

    LOOKUPS = [[1, 2], [5, 7], [8], [10]]
    ONEHOT = [f for group in LOOKUPS for f in group]
    GROUPS = [[0, 3, 6, 9], [12, 13, 14, 15], [16, 17, 18, 19], [20, 21, 22, 23], [4, 11], [24, 25, NF]]
    SLOTS = [f for group in GROUPS for f in group]
    GATHERED = [f for f in SLOTS if f != NF]
    PARTS = [[0, 1, 2], [3], [4, 5]]
    IN_PART = [sum(f != NF for g in part for f in GROUPS[g]) for part in PARTS]
    DENSE_SLOT = SLOTS.index(NF)
    NG, NO = len(GATHERED), len(ONEHOT)
    ROWS = tables[ONEHOT[0]].shape[0]
    CH = 8
    RP = ROWS // CH
    NL = len(LOOKUPS)
    AT = [sum(len(x) for x in LOOKUPS[:g]) for g in range(NL)]
    HOTS = 3
    GP = 8
    QG = QUADS // GP
    assert QG * 4 * F <= 512
    assert sorted(ONEHOT + SLOTS) == list(range(F)) and all(tables[f].shape[0] == ROWS for f in ONEHOT)

    def numbered(start, names):
        return {name: ((start + n) % 2, (start + n) // 2 + 1) for n, name in enumerate(names)}

    ID = [("ids", g) for g in range(NL)]
    ROWT = [[("rows", t, g) for g in range(len(GROUPS))] for t in range(2)]
    ORDER = ROWT[0][:3] + [("z", 1)] + ROWT[0][3:] + ID + [("z", 0)] + ROWT[1]
    AHEAD = ID
    PER = len(ORDER)
    BEFORE = numbered(0, AHEAD)
    first_order = [x for x in ORDER if x != ("z", 1)]
    last_order = ROWT[0][:3] + [("z", 1)] + ROWT[0][3:] + ROWT[1][:3] + [("z", 0)] + ROWT[1][3:]
    n1 = len(AHEAD) + len(first_order)
    FIRST = numbered(len(AHEAD), first_order)
    STEADY = numbered(n1, ORDER)
    LAST = numbered(n1 + PER * (SUPER - 2), last_order)
    AFTER = numbered(n1 + PER * (SUPER - 2) + len(last_order), [("z", 1)])
    assert PER % 2 == 0

    def fill_of(s, name):
        if isinstance(s, int):
            if s < 0:
                return BEFORE[name]
            if s == 0:
                return FIRST[name]
            if s == SUPER - 1:
                return LAST[name]
            if s == SUPER:
                return AFTER[name]
        bank, count = STEADY[name]
        return bank, (s - 1) * (PER // 2) + count

    ctx = ExitStack()
    with ctx:
        def sb(name, shape, dt):
            return ctx.enter_context(nc.sbuf_tensor(name, shape, dt))

        def pb(name, shape, dt):
            return ctx.enter_context(nc.psum_tensor(name, shape, dt))

        def sem(name):
            return ctx.enter_context(nc.semaphore(name))

        gather_ids = sb("gather_ids", [P, 2, NF], i32)
        ids_rows = sb("ids_rows", [P, SB], fp16)
        minus_row = sb("minus_row", [P, 1], fp32)
        ident = sb("ident", [P, P], fp32)
        ident16 = sb("ident16", [P, P], fp16)
        table_hi = sb("table_hi", [RP, NO, CH, D], f32r)
        table_lo = sb("table_lo", [RP, NO, CH, D], f32r)
        ids_all = sb("ids_all", [P, NL, 2, SB], fp16)
        onehot = sb("onehot", [RP, HOTS, CH, SB], f32r)
        rows = sb("rows", [P, 2, NG + 1, D], fp32)
        features = sb("features", [P, 2, SB, FP], fp32)
        raw = features[:, 1].rearrange("p c f -> p (c f)")
        table_raw = raw[0:RP, 0:NO * CH * D].rearrange("p (o k d) -> p o k d", o=NO, k=CH)
        w1z_raw = raw[0:ZK, NO * CH * D:NO * CH * D + ZC * N1].rearrange("p (c n) -> p c n", c=ZC)
        raw_words = features[:, 0].rearrange("p c f -> p (c f)")
        ids_raw = raw_words[:, 0:TILES * NF].bitcast(i32).rearrange("p (t f) -> p t f", t=TILES)
        ids_half = raw_words[:, TILES * NF:TILES * NF + SB // 2].bitcast(fp16).rearrange("p (t k) -> p t k", t=2)[:, :, 0:SUPER * NO]
        denseT = sb("denseT", [P, 2, SB], fp32)
        grams = sb("grams", [P, F, QUADS], fp32)
        gramsT = sb("gramsT", [P, F, FP], fp32)
        z = sb("z", [P, 2, PAIRS], fp32)
        zT_hi = sb("zT_hi", [ZK, ZC, SB], f32r)
        zT_lo = sb("zT_lo", [ZK, ZC, SB], f32r)
        h1 = sb("h1", [P, N1 // P, SB], fp32)
        h2 = sb("h2", [P, N2 // P, SB], fp32)
        y = sb("y", [P, TILES], fp32)
        w1z_hi = sb("w1z_hi", [ZK, ZC, N1], f32r)
        w1z_lo = sb("w1z_lo", [ZK, ZC, N1], f32r)
        w1d = sb("w1d", [P, N1], fp32)
        w2_sb = sb("w2_sb", [P, N1 // P, N2], fp32)
        w3_sb = sb("w3_sb", [P, N2 // P], fp32)
        b1_sb = sb("b1_sb", [P, N1 // P], fp32)
        b2_sb = sb("b2_sb", [P, N2 // P], fp32)

        fillp = [pb(f"fillp{i}", [P, 512], fp32) for i in range(2)]
        lookp = pb("lookp", [P, 512], fp32)
        gramp = [pb(f"gramp{i}", [P, 512], fp32) for i in range(3)]
        mlpp = pb("mlpp", [P, 2, 512], fp32)
        idsp = mlpp[0:SUPER * NO, 0, 0:P].bitcast(fp16)

        ids_loaded = sem("ids_loaded")
        gather_ids_loaded = [sem(f"gather_ids_loaded{i}") for i in range(2)]
        table_loaded = [sem(f"table_loaded{k}") for k in range(NO)]
        w1z_loaded = sem("w1z_loaded")
        weights_loaded = sem("weights_loaded")
        rows_gathered = [[sem(f"rows_gathered{i}_{part}") for part in range(len(PARTS))] for i in range(2)]
        dense_loaded = [sem(f"dense_loaded{i}") for i in range(2)]
        gather_begun = sem("gather_begun")
        out_stored = sem("out_stored")
        zeroed = sem("zeroed")
        ids_rows_zeroed = sem("ids_rows_zeroed")
        ident_made = sem("ident_made")
        ident16_made = sem("ident16_made")
        ids_cast = sem("ids_cast")
        ids_transposed = sem("ids_transposed")
        ids_ready = sem("ids_ready")
        hi_ready = sem("hi_ready")
        lo_ready = sem("lo_ready")
        w1z_hi_ready = sem("w1z_hi_ready")
        w1z_lo_ready = sem("w1z_lo_ready")
        zT_hi_ready = sem("zT_hi_ready")
        pads_zeroed = sem("pads_zeroed")
        onehot_built = sem("onehot_built")
        looked_up = sem("looked_up")
        lookup_drained = sem("lookup_drained")
        rows_numbered = sem("rows_numbered")
        bank_filled = [sem(f"bank_filled{i}") for i in range(2)]
        bank_drained = [sem(f"bank_drained{i}") for i in range(2)]
        gram_filled = sem("gram_filled")
        gram_drained = sem("gram_drained")
        gram_turned = sem("gram_turned")
        z_packed = sem("z_packed")
        h1_filled = sem("h1_filled")
        h1_ready = sem("h1_ready")
        h2_filled = sem("h2_filled")
        h2_ready = sem("h2_ready")
        y_filled = sem("y_filled")
        y_ready = sem("y_ready")

        block = ctx.enter_context(nc.Block())

        def wait_filled(eng, s, name):
            bank, count = fill_of(s, name)
            eng.wait_ge(bank_filled[bank], count)
            return bank

        def wait_drained(eng, s, name):
            bank, count = fill_of(s, name)
            eng.wait_ge(bank_drained[bank], count)

        def run_of(fs):
            return slice(fs[0], fs[-1] + 1, fs[1] - fs[0] if len(fs) > 1 else 1)

        dense_v = dense.rearrange("(p t) d -> p t d", t=TILES)

        @block.sync
        def _(sp):
            ids_v = ids.rearrange("(p t) f -> p t f", t=TILES)

            def load_ids(t, tile):
                sp.dma_start(gather_ids[:, t, :], ids_v[:, tile, :]).then_inc(gather_ids_loaded[t], 16)

            load_ids(0, 0)
            sp.dma_start(ids_raw[:, :, :], ids_v).then_inc(ids_loaded, 16)
            load_ids(1, 1)

            def load_dense(t, tile):
                sp.dma_start(rows[:, t, DENSE_SLOT, :], dense_v[:, tile, :]).then_inc(dense_loaded[t], 16)

            for k, f in enumerate(ONEHOT):
                sp.dma_start(table_raw[:, k], tables[f].rearrange("(p k) d -> p k d", k=CH)).then_inc(table_loaded[k], 16)
                if k < 2:
                    load_dense(k, k)
            sp.dma_start(w1z_raw, w1[0:PAIRS, :].rearrange("(c p) n -> p c n", c=ZC)).then_inc(w1z_loaded, 16)
            sp.dma_start(w1d[:, :], w1[PAIRS:PAIRS + D, :]).then_inc(weights_loaded, 16)
            sp.dma_start(w2_sb[:, :, :], w2.rearrange("(c p) n -> p c n", p=P)).then_inc(weights_loaded, 16)
            sp.dma_start(w3_sb[:, :], w3.rearrange("(c p) o -> p (c o)", p=P),
                         allow_slow_non_contiguous=True).then_inc(weights_loaded, 16)
            sp.dma_start(b1_sb[:, :], b1.rearrange("(c p) -> p c", p=P),
                         allow_slow_non_contiguous=True).then_inc(weights_loaded, 16)
            sp.dma_start(b2_sb[:, :], b2.rearrange("(c p) -> p c", p=P),
                         allow_slow_non_contiguous=True).then_inc(weights_loaded, 16)
            with sp.Fori(1, SUPER) as s:
                for t in range(2):
                    wait_drained(sp, s - 1, ROWT[t][-1])
                    load_ids(t, bass.ds(s * 2 + t, 1))
                    load_dense(t, bass.ds(s * 2 + t, 1))
            sp.wait_ge(y_ready, SUPER)
            sp.dma_start(out.rearrange("(p t) o -> p (t o)", t=TILES), y[:, :]).then_inc(out_stored, 16)
            sp.wait_ge(out_stored, 16)

        WEIGHTS = 5 * 16

        @block.gpsimd
        def _(pool):
            pool.memset(ids_rows[:, :].bitcast(fp32), 0.0).then_inc(ids_rows_zeroed, 1)
            pool.wait_ge(zeroed, 1)
            pool.affine_select(out=ident[:, :], in_=ident[:, :], compare_op=ALU.not_equal, fill=1.0,
                               base=0, pattern=[[-1, P]], channel_multiplier=1).then_inc(ident_made, 1)
            pool.iota(minus_row[:, :], [[0, 1]], base=0, channel_multiplier=-CH,
                      allow_small_or_imprecise_dtypes=True).then_inc(rows_numbered, 1)

            def gather(t, s):
                pool.wait_ge(gather_ids_loaded[t], (s + 1) * 16)
                pool.sem_inc(gather_begun, 1)
                for part, groups in enumerate(PARTS):
                    for f in [f for g in groups for f in GROUPS[g] if f != NF]:
                        pool.indirect_dma_start(
                            rows[:, t, SLOTS.index(f), :], None, tables[f],
                            bass.IndirectOffsetOnAxis(ap=gather_ids[:, t, f:f + 1], axis=0)).then_inc(rows_gathered[t][part], 16)

            for t in range(2):
                gather(t, 0)
            with pool.Fori(1, SUPER) as s:
                for t in range(2):
                    wait_drained(pool, s - 1, ROWT[t][-1])
                    gather(t, s)

        @block.tensor
        def _(pe):
            def open_fill(s, name):
                bank, count = fill_of(s, name)
                if not isinstance(count, int) or count > 1:
                    pe.wait_ge(bank_drained[bank], count - 1)
                return bank

            def ids_fill(it, s, g):
                bank = open_fill(it, ("ids", g))
                for j in range(len(LOOKUPS[g])):
                    row = ident16[:, bass.ds(s * NO + AT[g] + j, 1)].to_broadcast([P, P])
                    last = pe.matmul(fillp[bank][:, j * SB:(j + 1) * SB], row, ids_rows[:, :], start=True, stop=True)
                last.then_inc(bank_filled[bank], 1)

            def lookup_half(s, g, j, half):
                k = AT[g] + j
                if half == 0:
                    pe.wait_ge(onehot_built, s * NO + k + 1)
                    if isinstance(s, int) and s == 0:
                        pe.wait_ge(hi_ready, k + 1)
                elif isinstance(s, int) and s == 0:
                    pe.wait_ge(lo_ready, k + 1)
                if j == 0 and half == 0 and not (isinstance(s, int) and s == 0 and g == 0):
                    pe.wait_ge(lookup_drained, s * NL + g)
                table = (table_hi, table_lo)[half]
                for c in range(CH):
                    last = pe.matmul(lookp[:, j * SB:(j + 1) * SB], table[:, k, c, :], onehot[:, k % HOTS, c, :],
                                     start=(half == 0 and c == 0), stop=(half == 1 and c == CH - 1))
                if half == 1:
                    last.then_inc(looked_up, 1)

            def lookup(s, g):
                for j in range(len(LOOKUPS[g])):
                    for half in range(2):
                        lookup_half(s, g, j, half)

            def rows_fill(s, t, g):
                bank = open_fill(s, ("rows", t, g))
                part = [g in groups for groups in PARTS].index(True)
                if g == PARTS[part][0]:
                    pe.wait_ge(rows_gathered[t][part], (s + 1) * (16 * IN_PART[part]))
                if g == len(GROUPS) - 1:
                    pe.wait_ge(dense_loaded[t], (s + 1) * 16)
                slot = sum(len(x) for x in GROUPS[:g])
                for j in range(len(GROUPS[g])):
                    last = pe.transpose(fillp[bank][:, j * D:(j + 1) * D], rows[:, t, slot + j, :], ident[:, :])
                last.then_inc(bank_filled[bank], 1)

            def z_fill(it, s, t):
                bank = open_fill(it, ("z", t))
                pe.wait_ge(z_packed, s * 2 + t + 1)
                for c in range(ZC):
                    last = pe.transpose(fillp[bank][0:ZK, c * P:(c + 1) * P], z[:, t, c * ZK:(c + 1) * ZK], ident[:, :])
                last.then_inc(bank_filled[bank], 1)

            def gram(s, parity, t):
                for name in ROWT[t][-2:]:
                    wait_drained(pe, s, name)
                pe.wait_ge(lookup_drained, s * NL + NL)
                for g in range(GP):
                    if g >= 3:
                        pe.wait_ge(gram_drained, (s * 2 + t) * GP + g - 2)
                    elif g == 0 and not (isinstance(s, int) and s == 0 and t == 0):
                        pe.wait_ge(gram_drained, (s * 2 + t) * GP)
                    for q in range(QG):
                        at = t * P + 4 * (g * QG + q)
                        quad = features[:, parity, at:at + 4, :]
                        last = pe.matmul(gramp[g % 3][:, q * 4 * F:(q + 1) * 4 * F],
                                         quad.rearrange("d j f -> d (j f)"), quad[:, :, 0:F], start=True, stop=True)
                    last.then_inc(gram_filled, 1)

            def units(n):
                return mlpp[:, n // 2, n % 2 * SB:(n % 2 + 1) * SB]

            def layer1_dense(parity, half):
                for n in (2 * half, 2 * half + 1):
                    pe.matmul(units(n), w1d[:, n * P:(n + 1) * P], denseT[:, parity, :],
                              start=(n % 2 == 0), stop=False, skip_group_check=True)

            def layer1(it, n):
                if n == 0:
                    wait_drained(pe, it, ("z", 1))
                for c in range(ZC):
                    for w, zT in ((w1z_hi, zT_hi), (w1z_hi, zT_lo), (w1z_lo, zT_hi)):
                        last = pe.matmul(units(n), w[:, c, n * P:(n + 1) * P], zT[:, c, :],
                                         start=False, stop=(c == ZC - 1 and w is w1z_lo), skip_group_check=True)
                if n % 2 == 1:
                    last.then_inc(h1_filled, 1)

            def layer2(u, n):
                for c in range(N1 // P):
                    if n == 0 and c % 2 == 0:
                        pe.wait_ge(h1_ready, u * 2 + c // 2 + 1)
                    last = pe.matmul(units(n), w2_sb[:, c, n * P:(n + 1) * P], h1[:, c, :],
                                     start=(c == 0), stop=(c == N1 // P - 1))
                if n == 1:
                    last.then_inc(h2_filled, 1)

            def layer3(u):
                pe.wait_ge(h2_ready, u + 1)
                for t in range(2):
                    for c in range(N2 // P):
                        last = pe.matmul(mlpp[:, 1, t:t + 1], h2[:, c, t * P:(t + 1) * P], w3_sb[:, c:c + 1],
                                         start=(c == 0), stop=(c == N2 // P - 1))
                last.then_inc(y_filled, 1)

            def next_layer1(u):
                pe.wait_ge(y_ready, u + 1)

            def superblock(s, parity):
                mlp = not (isinstance(s, int) and s == 0)
                ahead = not (isinstance(s, int) and s == SUPER - 1)
                rows_fill(s, 0, 0)
                rows_fill(s, 0, 1)
                if mlp:
                    layer1_dense(1 - parity, 0)
                rows_fill(s, 0, 2)
                if mlp:
                    layer1_dense(1 - parity, 1)
                    z_fill(s, s - 1, 1)
                rows_fill(s, 0, 3)
                rows_fill(s, 0, 4)
                if mlp:
                    layer1(s, 0)
                rows_fill(s, 0, 5)
                if mlp:
                    layer1(s, 1)
                    layer1(s, 2)
                if ahead:
                    ids_fill(s, s + 1, 0)
                if mlp:
                    layer1(s, 3)
                if ahead:
                    ids_fill(s, s + 1, 1)
                gram(s, parity, 0)
                if not ahead:
                    rows_fill(s, 1, 0)
                    rows_fill(s, 1, 1)
                    layer2(s - 1, 0)
                    rows_fill(s, 1, 2)
                    z_fill(s, s, 0)
                    for g in (3, 4, 5):
                        rows_fill(s, 1, g)
                    gram(s, parity, 1)
                    layer2(s - 1, 1)
                    layer3(s - 1)
                    z_fill(SUPER, s, 1)
                    next_layer1(s - 1)
                    layer1_dense(parity, 0)
                    layer1_dense(parity, 1)
                    for n in range(N1 // P):
                        layer1(SUPER, n)
                    layer2(s, 0)
                    layer2(s, 1)
                    layer3(s)
                    return
                lookup(s + 1, 0)
                if mlp:
                    layer2(s - 1, 0)
                ids_fill(s, s + 1, 2)
                ids_fill(s, s + 1, 3)
                if mlp:
                    layer2(s - 1, 1)
                z_fill(s, s, 0)
                lookup(s + 1, 1)
                rows_fill(s, 1, 0)
                rows_fill(s, 1, 1)
                lookup_half(s + 1, 2, 0, 0)
                rows_fill(s, 1, 2)
                rows_fill(s, 1, 3)
                lookup_half(s + 1, 2, 0, 1)
                rows_fill(s, 1, 4)
                rows_fill(s, 1, 5)
                if mlp:
                    layer3(s - 1)
                gram(s, parity, 1)
                if mlp:
                    next_layer1(s - 1)
                lookup(s + 1, 3)

            pe.wait_ge(ident16_made, 1)
            pe.wait_ge(ids_cast, 1)
            for t in range(2):
                last = pe.transpose(idsp[:, t * P:(t + 1) * P], ids_half[:, t, :], ident16[:, :])
            last.then_inc(ids_transposed, 1)
            pe.wait_ge(ids_ready, 1)
            pe.wait_ge(ident_made, 1)
            for g in range(NL):
                ids_fill(-1, 0, g)
            for g in range(NL):
                lookup(0, g)
            pe.wait_ge(pads_zeroed, 2)
            superblock(0, 0)
            pe.wait_ge(w1z_hi_ready, 1)
            pe.wait_ge(w1z_lo_ready, 1)
            pe.wait_ge(weights_loaded, WEIGHTS)
            with pe.Fori(0, SUPER // 2 - 1) as i:
                superblock(i * 2 + 1, 1)
                superblock(i * 2 + 2, 0)
            superblock(SUPER - 1, 1)

        @block.scalar
        def _(act):
            def copy(o, i):
                return act.activation(o, i, ACT.Copy)

            def drain_rows(s, parity, t, g):
                bank = wait_filled(act, s, ("rows", t, g))
                dst = features[:, parity, t * P:(t + 1) * P, :].rearrange("d (q j) f -> d f j q", j=4)
                src = fillp[bank][:, :].rearrange("d (f j q) -> d f j q", j=4, q=QUADS)
                fs = GROUPS[g]
                if NF in fs:
                    copy(dst[:, run_of(fs)], src[:, 0:len(fs)])
                    at = fs.index(NF) * P
                    last = copy(denseT[:, parity, t * P:(t + 1) * P], fillp[bank][:, at:at + P])
                else:
                    last = copy(dst[:, run_of(fs)], src[:, 0:len(fs)])
                last.then_inc(bank_drained[bank], 1)

            def drain_gram(s, t, g):
                act.wait_ge(gram_filled, s * (2 * GP) + GP * t + g + 1)
                for j in range(4):
                    src = gramp[g % 3][32 * j:32 * j + 32, 0:QG * 4 * F].rearrange("f (q c) -> f c q", q=QG)
                    last = copy(grams[32 * j:32 * j + 32, :, g * QG:(g + 1) * QG], src[:, j * F:(j + 1) * F])
                last.then_inc(gram_drained, 1)

            def drain_ids(it, g):
                bank = wait_filled(act, it, ("ids", g))
                n = len(LOOKUPS[g]) * SB
                act.activation(ids_all[:, g].rearrange("p j c -> p (j c)")[:, 0:n], fillp[bank][:, 0:n], ACT.Identity,
                               bias=minus_row[:, :]).then_inc(bank_drained[bank], 1)

            def drain_lookup(s, parity, g):
                act.wait_ge(looked_up, s * NO + AT[g] + len(LOOKUPS[g]))
                dst = features[:, parity, :, :].rearrange("d c f -> d f c")[:, run_of(LOOKUPS[g])]
                n = len(LOOKUPS[g])
                copy(dst, lookp[:, 0:n * SB].rearrange("d (f c) -> d f c", f=n)).then_inc(lookup_drained, 1)

            def high_z(it, t):
                bank = wait_filled(act, it, ("z", t))
                copy(zT_hi[:, :, t * P:(t + 1) * P],
                     fillp[bank][0:ZK, 0:ZC * P].rearrange("k (c n) -> k c n", c=ZC)).then_inc(zT_hi_ready, 1)

            def relu1(u, half):
                act.wait_ge(h1_filled, u * 2 + half + 1)
                for n in (2 * half, 2 * half + 1):
                    last = act.activation(h1[:, n, :], mlpp[:, half, n % 2 * SB:(n % 2 + 1) * SB],
                                          ACT.Relu, bias=b1_sb[:, n:n + 1])
                last.then_inc(h1_ready, 1)

            def relu2(u):
                act.wait_ge(h2_filled, u + 1)
                for n in range(N2 // P):
                    last = act.activation(h2[:, n, :], mlpp[:, 0, n * SB:(n + 1) * SB],
                                          ACT.Relu, bias=b2_sb[:, n:n + 1])
                last.then_inc(h2_ready, 1)

            def drain_grams(s, t):
                if not (isinstance(s, int) and s == 0 and t == 0):
                    act.wait_ge(gram_turned, s * 2 + t)
                for g in range(GP):
                    drain_gram(s, t, g)

            def superblock(s, parity):
                mlp = not (isinstance(s, int) and s == 0)
                ahead = not (isinstance(s, int) and s == SUPER - 1)
                for g in range(3):
                    drain_rows(s, parity, 0, g)
                if mlp:
                    high_z(s, 1)
                for g in (3, 4, 5):
                    drain_rows(s, parity, 0, g)
                if mlp:
                    relu1(s - 1, 0)
                if ahead:
                    drain_ids(s, 0)
                if mlp:
                    relu1(s - 1, 1)
                if ahead:
                    drain_ids(s, 1)
                drain_grams(s, 0)
                if not ahead:
                    for g in range(3):
                        drain_rows(s, parity, 1, g)
                    high_z(s, 0)
                    for g in (3, 4, 5):
                        drain_rows(s, parity, 1, g)
                    drain_grams(s, 1)
                    relu2(s - 1)
                    return
                drain_lookup(s + 1, 1 - parity, 0)
                drain_ids(s, 2)
                drain_ids(s, 3)
                if mlp:
                    relu2(s - 1)
                high_z(s, 0)
                drain_lookup(s + 1, 1 - parity, 1)
                for g in range(len(GROUPS)):
                    drain_rows(s, parity, 1, g)
                drain_lookup(s + 1, 1 - parity, 2)
                drain_grams(s, 1)
                if ahead:
                    drain_lookup(s + 1, 1 - parity, 3)

            act.wait_ge(rows_numbered, 1)
            act.wait_ge(ids_transposed, 1)
            act.wait_ge(ids_rows_zeroed, 1)
            copy(ids_rows[0:SUPER * NO, :].rearrange("k (t q j) -> k t j q", j=4, q=QUADS),
                 idsp.rearrange("k (t j q) -> k t j q", j=4, q=QUADS)).then_inc(ids_ready, 1)
            for k in range(NO):
                if k in AT:
                    drain_ids(-1, AT.index(k))
                act.wait_ge(table_loaded[k], 16)
                copy(table_hi[:, k], table_raw[:, k]).then_inc(hi_ready, 1)
            act.wait_ge(w1z_loaded, 16)
            copy(w1z_hi[:, :, :], w1z_raw).then_inc(w1z_hi_ready, 1)
            for g in range(NL):
                drain_lookup(0, 0, g)
            act.wait_ge(lo_ready, NO)
            act.wait_ge(w1z_lo_ready, 1)
            superblock(0, 0)
            with act.Fori(0, SUPER // 2 - 1) as i:
                superblock(i * 2 + 1, 1)
                superblock(i * 2 + 2, 0)
            superblock(SUPER - 1, 1)
            high_z(SUPER, 1)
            relu1(SUPER - 1, 0)
            relu1(SUPER - 1, 1)
            relu2(SUPER - 1)

        @block.vector
        def _(dve):
            def build(it, s, k):
                g = max(x for x in range(NL) if AT[x] <= k)
                j = k - AT[g]
                if j == 0:
                    wait_drained(dve, it, ("ids", g))
                if k >= HOTS:
                    dve.wait_ge(looked_up, s * NO + k - HOTS + 1)
                elif k == 0 and not (isinstance(s, int) and s == 0):
                    dve.wait_ge(looked_up, s * NO)
                for c in range(CH):
                    last = dve.tensor_scalar(onehot[:, k % HOTS, c, :], ids_all[0:RP, g, j, :],
                                             float(c), None, ALU.is_equal)
                last.then_inc(onehot_built, 1)

            def pack(s, t):
                dve.wait_ge(gram_drained, (s * 2 + t + 1) * GP)
                if not (isinstance(s, int) and s == 0 and t == 0):
                    dve.wait_ge(z_packed, s * 2 + t)
                dve.transpose(gramsT[:, :, :].rearrange("p g f -> p (g f)"),
                              grams[:, :, :].rearrange("p g q -> p (g q)")).then_inc(gram_turned, 1)
                dve.wait_ge(gram_turned, s * 2 + t + 1)
                if not (isinstance(s, int) and s == 0):
                    wait_filled(dve, s - 1 if t == 0 else s, ("z", t))
                at = 0
                for i in range(F - 1):
                    n = F - 1 - i
                    last = dve.tensor_copy(z[:, t, at:at + n], gramsT[:, i, i + 1:F])
                    at += n
                last.then_inc(z_packed, 1)

            def low_z(it, n, t):
                bank, _ = fill_of(it, ("z", t))
                dve.wait_ge(zT_hi_ready, n)
                dve.tensor_tensor(zT_lo[:, :, t * P:(t + 1) * P],
                                  fillp[bank][0:ZK, 0:ZC * P].rearrange("k (c n) -> k c n", c=ZC),
                                  zT_hi[:, :, t * P:(t + 1) * P], ALU.subtract).then_inc(bank_drained[bank], 1)

            def y_copy(u):
                dve.wait_ge(y_filled, u + 1)
                dve.tensor_copy(y[:, bass.ds(u * 2, 2)], mlpp[:, 1, 0:2]).then_inc(y_ready, 1)

            def superblock(s):
                mlp = not (isinstance(s, int) and s == 0)
                ahead = not (isinstance(s, int) and s == SUPER - 1)
                if mlp:
                    low_z(s, s * 2, 1)
                if ahead:
                    for k in range(3):
                        build(s, s + 1, k)
                pack(s, 0)
                if ahead:
                    build(s, s + 1, 3)
                    build(s, s + 1, 4)
                low_z(s, s * 2 + 1, 0)
                if ahead:
                    build(s, s + 1, 5)
                if mlp and ahead:
                    y_copy(s - 1)
                pack(s, 1)
                if not ahead:
                    y_copy(s - 1)

            dve.memset(ident[:, :], 0.0).then_inc(zeroed, 1)
            dve.wait_ge(ident_made, 1)
            dve.tensor_copy(ident16[:, :], ident[:, :]).then_inc(ident16_made, 1)
            dve.wait_ge(ident16_made, 1)
            dve.wait_ge(ids_loaded, 16)
            for k, f in enumerate(ONEHOT):
                last = dve.tensor_copy(ids_half[:, :, k::NO], ids_raw[:, :, f].rearrange("p (s t) -> p t s", t=2))
            last.then_inc(ids_cast, 1)

            def split(k):
                dve.wait_ge(hi_ready, k + 1)
                dve.tensor_tensor(table_lo[:, k], table_raw[:, k], table_hi[:, k], ALU.subtract).then_inc(lo_ready, 1)

            for k in range(NO):
                split(k)
                build(-1, 0, k)
            dve.memset(features[:, 0, :, F:FP], 0.0).then_inc(pads_zeroed, 1)
            dve.wait_ge(w1z_hi_ready, 1)
            dve.tensor_tensor(w1z_lo[:, :, :], w1z_raw, w1z_hi[:, :, :], ALU.subtract).then_inc(w1z_lo_ready, 1)
            dve.wait_ge(lo_ready, NO)
            dve.wait_ge(w1z_lo_ready, 1)
            dve.memset(features[:, 1, :, F:FP], 0.0).then_inc(pads_zeroed, 1)
            superblock(0)
            with dve.Fori(0, SUPER // 2 - 1) as i:
                superblock(i * 2 + 1)
                superblock(i * 2 + 2)
            superblock(SUPER - 1)
            low_z(SUPER, SUPER * 2, 1)
            y_copy(SUPER - 1)


_TABLES = [f"tbl_{i}" for i in range(26)]
_INS = ["r_dense_x", "ids"] + _TABLES + ["W_top1", "b_top1", "W_top2", "b_top2", "W_top3"]


def kernel(**inputs):
    import numpy as _np
    import concourse.bacc as _bacc
    from concourse import mybir as _mybir
    from concourse.bass_utils import run_bass_kernel_spmd as _run

    nc = _bacc.Bacc("TRN2", target_bir_lowering=False, num_devices=1)
    arrays, args = {}, {}
    for name in _INS:
        a = _np.ascontiguousarray(inputs[name])
        arrays[f"in_{name}"] = a
        args[name] = nc.dram_tensor(f"in_{name}", a.shape, _mybir.dt.from_np(a.dtype), kind="ExternalInput").ap()
    out = nc.dram_tensor("out_y", (arrays["in_r_dense_x"].shape[0], 1), _mybir.dt.float32, kind="ExternalOutput").ap()
    dlrm_tower(nc, args["r_dense_x"], args["ids"], [args[n] for n in _TABLES],
               args["W_top1"], args["b_top1"], args["W_top2"], args["b_top2"], args["W_top3"], out)
    r = _run(nc, [arrays], core_ids=[0])
    return r.results[0]["out_y"]
```
